# Optimizing a Trainium2 kernel written in Bass

```python
import numpy as np
import jax
import jax.numpy as jnp

def _softmax(x, axis=-1):
    return jax.nn.softmax(x, axis=axis)

def _gelu(x):
    return jax.nn.gelu(x, approximate=True)

def _silu(x):
    return jax.nn.silu(x)

def _sigmoid(x):
    return jax.nn.sigmoid(x)

def _layernorm(x, axis=-1, eps=1e-05):
    m = jnp.mean(x, axis=axis, keepdims=True)
    v = jnp.var(x, axis=axis, keepdims=True)
    return (x - m) / jnp.sqrt(v + eps)

def _scatter_add(tgt, idx, src, axis=0):
    return tgt.at[idx].add(src)

def _segment_sum(src, seg, n):
    return jax.ops.segment_sum(src, seg, n)
kernel_name = 'mk_metaformer_d2_conv_nchw256_r4_a414dd'

def setup_inputs(seed: int=0):
    np.random.seed(seed)
    _w = jnp.asarray

    def _rec_inputs():
        import jax
        import jax.numpy as jnp
        _gk = jax.random.key(seed)
        x = 7.22e-05 + 1 * jax.random.normal(jax.random.fold_in(_gk, 1), (8, 64, 16, 16), jnp.float32)
        return x
    x = _rec_inputs()

    def _L0_conv_setup():
        import jax, jax.numpy as jnp
        import numpy as np
        BN_EPS = 1e-05
        K = 3

        def conv2d(x, w, b, pad):
            y = jax.lax.conv_general_dilated(x, w, window_strides=(1, 1), padding=[(pad, pad), (pad, pad)], dimension_numbers=('NCHW', 'OIHW', 'NCHW'))
            return y + b[None, :, None, None]

        def _dcn_bn_relu(x, w_off, b_off, w, b, gamma, beta, run_mean, run_var):
            B, C, H, W = x.shape
            KK = K * K
            om = conv2d(x, w_off, b_off, pad=1)
            dy, dx = (om[:, :KK], om[:, KK:2 * KK])
            mod = jax.nn.sigmoid(om[:, 2 * KK:])
            ky, kx = jnp.meshgrid(jnp.arange(K), jnp.arange(K), indexing='ij')
            base_y = jnp.arange(H, dtype=jnp.float32)[None, :, None] - 1.0 + ky.reshape(KK, 1, 1)
            base_x = jnp.arange(W, dtype=jnp.float32)[None, None, :] - 1.0 + kx.reshape(KK, 1, 1)
            py = base_y[None] + dy
            px = base_x[None] + dx
            y0 = jnp.floor(py)
            x0 = jnp.floor(px)
            fy = py - y0
            fx = px - x0
            y0 = y0.astype(jnp.int32)
            x0 = x0.astype(jnp.int32)
            x_flat = x.reshape(B, C, H * W)
            gather = jax.vmap(lambda xf, idx: xf[:, idx])

            def corner(yi, xi, wgt):
                valid = (yi >= 0) & (yi < H) & (xi >= 0) & (xi < W)
                idx = jnp.clip(yi, 0, H - 1) * W + jnp.clip(xi, 0, W - 1)
                val = gather(x_flat, idx)
                return val * (wgt * valid.astype(wgt.dtype))[:, None]
            sampled = corner(y0, x0, (1 - fy) * (1 - fx)) + corner(y0, x0 + 1, (1 - fy) * fx) + corner(y0 + 1, x0, fy * (1 - fx)) + corner(y0 + 1, x0 + 1, fy * fx)
            sampled = sampled * mod[:, None]
            O = w.shape[0]
            out = jnp.einsum('bckhw,ock->bohw', sampled, w.reshape(O, C, KK))
            out = out + b[None, :, None, None]
            inv = gamma / jnp.sqrt(run_var + BN_EPS)
            out = out * inv[None, :, None, None] + (beta - run_mean * inv)[None, :, None, None]
            return jax.nn.relu(out)
        key = jax.random.key(seed)
        ks = jax.random.split(key, 4)
        B, C, H, W, O = (8, 64, 16, 16, 64)
        x = jax.random.normal(ks[0], (B, C, H, W), dtype=jnp.float32)
        w_off = jax.random.normal(ks[1], (27, C, K, K), dtype=jnp.float32) * 0.01
        b_off = jnp.zeros((27,), dtype=jnp.float32)
        w = jax.random.normal(ks[2], (O, C, K, K), dtype=jnp.float32) * 0.05
        b = jnp.zeros((O,), dtype=jnp.float32)
        gamma = jnp.ones((O,), dtype=jnp.float32)
        beta = jnp.zeros((O,), dtype=jnp.float32)
        run_mean = jnp.zeros((O,), dtype=jnp.float32)
        run_var = jnp.ones((O,), dtype=jnp.float32)
        return {'x': x, 'w_off': w_off, 'b_off': b_off, 'w': w, 'b': b, 'gamma': gamma, 'beta': beta, 'run_mean': run_mean, 'run_var': run_var}
    _L0_conv_all = _L0_conv_setup()
    _L0_conv_in = {k: v for k, v in _L0_conv_all.items() if k in ('w_off', 'b_off', 'w', 'b', 'gamma', 'beta', 'run_mean', 'run_var')}
    del _L0_conv_all

    def _L0_ffn_setup():
        import jax, jax.numpy as jnp
        import numpy as np
        from jax import lax
        key = jax.random.key(seed)
        B, T, I, H = (16, 512, 64, 64)
        ks = jax.random.split(key, 13)
        s = 1.0 / np.sqrt(H)

        def w(k, shape):
            return jax.random.uniform(k, shape, jnp.float32, -s, s)
        return {'x': jax.random.normal(ks[0], (B, T, I), jnp.float32), 'U_i': w(ks[1], (I, H)), 'V_i': w(ks[2], (H, H)), 'b_i': w(ks[3], (H,)), 'U_f': w(ks[4], (I, H)), 'V_f': w(ks[5], (H, H)), 'b_f': w(ks[6], (H,)), 'U_c': w(ks[7], (I, H)), 'V_c': w(ks[8], (H, H)), 'b_c': w(ks[9], (H,)), 'U_o': w(ks[10], (I, H)), 'V_o': w(ks[11], (H, H)), 'b_o': w(ks[12], (H,))}
    _L0_ffn_all = _L0_ffn_setup()
    _L0_ffn_in = {k: v for k, v in _L0_ffn_all.items() if k in ('U_i', 'V_i', 'b_i', 'U_f', 'V_f', 'b_f', 'U_c', 'V_c', 'b_c', 'U_o', 'V_o', 'b_o')}
    del _L0_ffn_all

    def _L1_conv_setup():
        import jax, jax.numpy as jnp
        import numpy as np
        K = 3
        STRIDE = 1
        PAD = 1
        K2 = K * K

        def _conv2d(x, w, b):
            out = jax.lax.conv_general_dilated(x, w, window_strides=(STRIDE, STRIDE), padding=[(PAD, PAD), (PAD, PAD)], dimension_numbers=('NCHW', 'OIHW', 'NCHW'))
            return out + b[None, :, None, None]

        def _bilinear_sample(img, py, px):
            C, H, W = img.shape
            y0f = jnp.floor(py)
            x0f = jnp.floor(px)
            dy = py - y0f
            dx = px - x0f
            y0 = y0f.astype(jnp.int32)
            x0 = x0f.astype(jnp.int32)

            def gather(yi, xi):
                valid = (yi >= 0) & (yi < H) & (xi >= 0) & (xi < W)
                yc = jnp.clip(yi, 0, H - 1)
                xc = jnp.clip(xi, 0, W - 1)
                v = img[:, yc, xc]
                return v * valid[None].astype(img.dtype)
            v00 = gather(y0, x0)
            v01 = gather(y0, x0 + 1)
            v10 = gather(y0 + 1, x0)
            v11 = gather(y0 + 1, x0 + 1)
            w00 = (1 - dy) * (1 - dx)
            w01 = (1 - dy) * dx
            w10 = dy * (1 - dx)
            w11 = dy * dx
            return v00 * w00[None] + v01 * w01[None] + v10 * w10[None] + v11 * w11[None]

        def _deform_conv_single(x, offset, mask, w):
            C, H, W = x.shape
            Ho, Wo = (mask.shape[1], mask.shape[2])
            off = offset.reshape(K2, 2, Ho, Wo)
            ky, kx = jnp.meshgrid(jnp.arange(K), jnp.arange(K), indexing='ij')
            base_y = (jnp.arange(Ho) * STRIDE - PAD)[None, :, None] + ky.reshape(K2, 1, 1)
            base_x = (jnp.arange(Wo) * STRIDE - PAD)[None, None, :] + kx.reshape(K2, 1, 1)
            py = base_y.astype(x.dtype) + off[:, 0]
            px = base_x.astype(x.dtype) + off[:, 1]
            sampled = _bilinear_sample(x, py, px) * mask[None]
            return jnp.einsum('ckhw,ock->ohw', sampled, w.reshape(w.shape[0], C, K2))
        key = jax.random.key(seed)
        k1, k2, k3, k4 = jax.random.split(key, 4)
        B, C, H, W, O = (2, 64, 32, 32, 64)
        x = jax.random.normal(k1, (B, C, H, W), jnp.float32)
        offset_w = jax.random.normal(k2, (3 * K2, C, K, K), jnp.float32) * 0.01
        offset_b = jax.random.normal(k3, (3 * K2,), jnp.float32) * 0.1
        dcn_w = jax.random.normal(k4, (O, C, K, K), jnp.float32) * (1.0 / np.sqrt(C * K2))
        return {'x': x, 'offset_w': offset_w, 'offset_b': offset_b, 'dcn_w': dcn_w}
    _L1_conv_all = _L1_conv_setup()
    _L1_conv_in = {k: v for k, v in _L1_conv_all.items() if k in ('offset_w', 'offset_b', 'dcn_w')}
    del _L1_conv_all

    def _L1_ffn_setup():
        import jax, jax.numpy as jnp
        import numpy as np
        N_EXPERTS = 8
        TOP_K = 2
        key = jax.random.key(seed)
        ks = jax.random.split(key, 5)
        B, T, C, E, H = (8, 512, 64, 8, 682)
        scale = 1.0 / np.sqrt(C)
        return {'x': jax.random.normal(ks[0], (B, T, C), dtype=jnp.float32), 'router_w': jax.random.normal(ks[1], (E, C), dtype=jnp.float32) * scale, 'w1': jax.random.normal(ks[2], (E, H, C), dtype=jnp.float32) * scale, 'w2': jax.random.normal(ks[3], (E, C, H), dtype=jnp.float32) * (1.0 / np.sqrt(H)), 'w3': jax.random.normal(ks[4], (E, H, C), dtype=jnp.float32) * scale}
    _L1_ffn_all = _L1_ffn_setup()
    _L1_ffn_in = {k: v for k, v in _L1_ffn_all.items() if k in ('router_w', 'w1', 'w2', 'w3')}
    del _L1_ffn_all
    return {'x': x, 'L0_conv_w_off': _L0_conv_in['w_off'], 'L0_conv_b_off': _L0_conv_in['b_off'], 'L0_conv_w': _L0_conv_in['w'], 'L0_conv_b': _L0_conv_in['b'], 'L0_conv_gamma': _L0_conv_in['gamma'], 'L0_conv_beta': _L0_conv_in['beta'], 'L0_conv_run_mean': _L0_conv_in['run_mean'], 'L0_conv_run_var': _L0_conv_in['run_var'], 'L0_ffn_U_i': _L0_ffn_in['U_i'], 'L0_ffn_V_i': _L0_ffn_in['V_i'], 'L0_ffn_b_i': _L0_ffn_in['b_i'], 'L0_ffn_U_f': _L0_ffn_in['U_f'], 'L0_ffn_V_f': _L0_ffn_in['V_f'], 'L0_ffn_b_f': _L0_ffn_in['b_f'], 'L0_ffn_U_c': _L0_ffn_in['U_c'], 'L0_ffn_V_c': _L0_ffn_in['V_c'], 'L0_ffn_b_c': _L0_ffn_in['b_c'], 'L0_ffn_U_o': _L0_ffn_in['U_o'], 'L0_ffn_V_o': _L0_ffn_in['V_o'], 'L0_ffn_b_o': _L0_ffn_in['b_o'], 'L1_conv_offset_w': _L1_conv_in['offset_w'], 'L1_conv_offset_b': _L1_conv_in['offset_b'], 'L1_conv_dcn_w': _L1_conv_in['dcn_w'], 'L1_ffn_router_w': _L1_ffn_in['router_w'], 'L1_ffn_w1': _L1_ffn_in['w1'], 'L1_ffn_w2': _L1_ffn_in['w2'], 'L1_ffn_w3': _L1_ffn_in['w3']}

def reference(x, L0_conv_w_off, L0_conv_b_off, L0_conv_w, L0_conv_b, L0_conv_gamma, L0_conv_beta, L0_conv_run_mean, L0_conv_run_var, L0_ffn_U_i, L0_ffn_V_i, L0_ffn_b_i, L0_ffn_U_f, L0_ffn_V_f, L0_ffn_b_f, L0_ffn_U_c, L0_ffn_V_c, L0_ffn_b_c, L0_ffn_U_o, L0_ffn_V_o, L0_ffn_b_o, L1_conv_offset_w, L1_conv_offset_b, L1_conv_dcn_w, L1_ffn_router_w, L1_ffn_w1, L1_ffn_w2, L1_ffn_w3):
    import jax
    import jax.numpy as jnp

    def _L0_conv_ref(x, w_off, b_off, w, b, gamma, beta, run_mean, run_var):
        import jax, jax.numpy as jnp
        import numpy as np
        BN_EPS = 1e-05
        K = 3

        def conv2d(x, w, b, pad):
            y = jax.lax.conv_general_dilated(x, w, window_strides=(1, 1), padding=[(pad, pad), (pad, pad)], dimension_numbers=('NCHW', 'OIHW', 'NCHW'))
            return y + b[None, :, None, None]

        def _dcn_bn_relu(x, w_off, b_off, w, b, gamma, beta, run_mean, run_var):
            B, C, H, W = x.shape
            KK = K * K
            om = conv2d(x, w_off, b_off, pad=1)
            dy, dx = (om[:, :KK], om[:, KK:2 * KK])
            mod = jax.nn.sigmoid(om[:, 2 * KK:])
            ky, kx = jnp.meshgrid(jnp.arange(K), jnp.arange(K), indexing='ij')
            base_y = jnp.arange(H, dtype=jnp.float32)[None, :, None] - 1.0 + ky.reshape(KK, 1, 1)
            base_x = jnp.arange(W, dtype=jnp.float32)[None, None, :] - 1.0 + kx.reshape(KK, 1, 1)
            py = base_y[None] + dy
            px = base_x[None] + dx
            y0 = jnp.floor(py)
            x0 = jnp.floor(px)
            fy = py - y0
            fx = px - x0
            y0 = y0.astype(jnp.int32)
            x0 = x0.astype(jnp.int32)
            x_flat = x.reshape(B, C, H * W)
            gather = jax.vmap(lambda xf, idx: xf[:, idx])

            def corner(yi, xi, wgt):
                valid = (yi >= 0) & (yi < H) & (xi >= 0) & (xi < W)
                idx = jnp.clip(yi, 0, H - 1) * W + jnp.clip(xi, 0, W - 1)
                val = gather(x_flat, idx)
                return val * (wgt * valid.astype(wgt.dtype))[:, None]
            sampled = corner(y0, x0, (1 - fy) * (1 - fx)) + corner(y0, x0 + 1, (1 - fy) * fx) + corner(y0 + 1, x0, fy * (1 - fx)) + corner(y0 + 1, x0 + 1, fy * fx)
            sampled = sampled * mod[:, None]
            O = w.shape[0]
            out = jnp.einsum('bckhw,ock->bohw', sampled, w.reshape(O, C, KK))
            out = out + b[None, :, None, None]
            inv = gamma / jnp.sqrt(run_var + BN_EPS)
            out = out * inv[None, :, None, None] + (beta - run_mean * inv)[None, :, None, None]
            return jax.nn.relu(out)
        return _dcn_bn_relu(x, w_off, b_off, w, b, gamma, beta, run_mean, run_var)

    def _L0_ffn_ref(x, U_i, V_i, b_i, U_f, V_f, b_f, U_c, V_c, b_c, U_o, V_o, b_o):
        import jax, jax.numpy as jnp
        import numpy as np
        from jax import lax
        B, T, _ = x.shape
        H = U_i.shape[1]
        xt = jnp.swapaxes(x, 0, 1)
        xi = xt @ U_i + b_i
        xf = xt @ U_f + b_f
        xg = xt @ U_c + b_c
        xo = xt @ U_o + b_o
        h0 = jnp.zeros((B, H), x.dtype)
        c0 = jnp.zeros((B, H), x.dtype)

        def step(carry, xs):
            h, c = carry
            xi_t, xf_t, xg_t, xo_t = xs
            i_t = jax.nn.sigmoid(xi_t + h @ V_i)
            f_t = jax.nn.sigmoid(xf_t + h @ V_f)
            g_t = jnp.tanh(xg_t + h @ V_c)
            o_t = jax.nn.sigmoid(xo_t + h @ V_o)
            c_new = h * c + i_t * g_t
            h_new = o_t * jnp.tanh(c_new)
            return ((h_new, c_new), h_new)
        (_, _), hs = lax.scan(step, (h0, c0), (xi, xf, xg, xo))
        return jnp.swapaxes(hs, 0, 1)

    def _L1_conv_ref(x, offset_w, offset_b, dcn_w):
        import jax, jax.numpy as jnp
        import numpy as np
        K = 3
        STRIDE = 1
        PAD = 1
        K2 = K * K

        def _conv2d(x, w, b):
            out = jax.lax.conv_general_dilated(x, w, window_strides=(STRIDE, STRIDE), padding=[(PAD, PAD), (PAD, PAD)], dimension_numbers=('NCHW', 'OIHW', 'NCHW'))
            return out + b[None, :, None, None]

        def _bilinear_sample(img, py, px):
            C, H, W = img.shape
            y0f = jnp.floor(py)
            x0f = jnp.floor(px)
            dy = py - y0f
            dx = px - x0f
            y0 = y0f.astype(jnp.int32)
            x0 = x0f.astype(jnp.int32)

            def gather(yi, xi):
                valid = (yi >= 0) & (yi < H) & (xi >= 0) & (xi < W)
                yc = jnp.clip(yi, 0, H - 1)
                xc = jnp.clip(xi, 0, W - 1)
                v = img[:, yc, xc]
                return v * valid[None].astype(img.dtype)
            v00 = gather(y0, x0)
            v01 = gather(y0, x0 + 1)
            v10 = gather(y0 + 1, x0)
            v11 = gather(y0 + 1, x0 + 1)
            w00 = (1 - dy) * (1 - dx)
            w01 = (1 - dy) * dx
            w10 = dy * (1 - dx)
            w11 = dy * dx
            return v00 * w00[None] + v01 * w01[None] + v10 * w10[None] + v11 * w11[None]

        def _deform_conv_single(x, offset, mask, w):
            C, H, W = x.shape
            Ho, Wo = (mask.shape[1], mask.shape[2])
            off = offset.reshape(K2, 2, Ho, Wo)
            ky, kx = jnp.meshgrid(jnp.arange(K), jnp.arange(K), indexing='ij')
            base_y = (jnp.arange(Ho) * STRIDE - PAD)[None, :, None] + ky.reshape(K2, 1, 1)
            base_x = (jnp.arange(Wo) * STRIDE - PAD)[None, None, :] + kx.reshape(K2, 1, 1)
            py = base_y.astype(x.dtype) + off[:, 0]
            px = base_x.astype(x.dtype) + off[:, 1]
            sampled = _bilinear_sample(x, py, px) * mask[None]
            return jnp.einsum('ckhw,ock->ohw', sampled, w.reshape(w.shape[0], C, K2))
        out = _conv2d(x, offset_w, offset_b)
        o1, o2, mask_raw = jnp.split(out, 3, axis=1)
        offset = jnp.concatenate([o1, o2], axis=1)
        mask = jax.nn.sigmoid(mask_raw)
        f = jax.vmap(_deform_conv_single, in_axes=(0, 0, 0, None))
        return f(x, offset, mask, dcn_w)

    def _L1_ffn_ref(x, router_w, w1, w2, w3):
        import jax, jax.numpy as jnp
        import numpy as np
        N_EXPERTS = 8
        TOP_K = 2
        B, T, C = x.shape
        flat = x.reshape(-1, C)
        logits = flat @ router_w.T
        probs = jax.nn.softmax(logits, axis=-1)
        topk_probs, topk_idx = jax.lax.top_k(probs, TOP_K)
        topk_probs = topk_probs / (jnp.sum(topk_probs, axis=-1, keepdims=True) + 1e-09)
        onehot = jax.nn.one_hot(topk_idx, N_EXPERTS, dtype=flat.dtype)
        gates = jnp.einsum('nk,nke->ne', topk_probs, onehot)
        h1 = jnp.einsum('nc,ehc->neh', flat, w1)
        h3 = jnp.einsum('nc,ehc->neh', flat, w3)
        h = jax.nn.silu(h1) * h3
        y = jnp.einsum('neh,ech->nec', h, w2)
        out = jnp.einsum('ne,nec->nc', gates, y)
        return out.reshape(B, T, C)

    def _gn(v, G=32, eps=1e-05):
        B_, C_, H_, W_ = v.shape
        g = v.reshape(B_, G, C_ // G, H_, W_)
        m = jnp.mean(g, axis=(2, 3, 4), keepdims=True)
        s = jnp.var(g, axis=(2, 3, 4), keepdims=True)
        return ((g - m) / jnp.sqrt(s + eps)).reshape(v.shape)

    def _ln_c(v, eps=1e-06):
        m = jnp.mean(v, axis=1, keepdims=True)
        s = jnp.var(v, axis=1, keepdims=True)
        return (v - m) / jnp.sqrt(s + eps)

    def _ln_t(v, eps=1e-05):
        m = jnp.mean(v, axis=-1, keepdims=True)
        s = jnp.var(v, axis=-1, keepdims=True)
        return (v - m) / jnp.sqrt(s + eps)

    def _to_tokens(v):
        B_, C_, H_, W_ = v.shape
        return v.reshape(B_, C_, H_ * W_).transpose(0, 2, 1)

    def _from_tokens(t, like):
        B_, C_, H_, W_ = like.shape
        return t.transpose(0, 2, 1).reshape(B_, C_, H_, W_)
    x = x + _L0_conv_ref(_ln_c(x), L0_conv_w_off, L0_conv_b_off, L0_conv_w, L0_conv_b, L0_conv_gamma, L0_conv_beta, L0_conv_run_mean, L0_conv_run_var)
    t = _to_tokens(x)
    t = t + _L0_ffn_ref(_ln_t(t), L0_ffn_U_i, L0_ffn_V_i, L0_ffn_b_i, L0_ffn_U_f, L0_ffn_V_f, L0_ffn_b_f, L0_ffn_U_c, L0_ffn_V_c, L0_ffn_b_c, L0_ffn_U_o, L0_ffn_V_o, L0_ffn_b_o)
    x = _from_tokens(t, x)
    x = x + _L1_conv_ref(_ln_c(x), L1_conv_offset_w, L1_conv_offset_b, L1_conv_dcn_w)
    t = _to_tokens(x)
    t = t + _L1_ffn_ref(_ln_t(t), L1_ffn_router_w, L1_ffn_w1, L1_ffn_w2, L1_ffn_w3)
    x = _from_tokens(t, x)
    return x

_drawn_inputs = setup_inputs


def setup_inputs(seed=0):
    import zlib

    import numpy as np

    out = dict(_drawn_inputs(seed))
    spreads = {'L0_conv_b_off': (0.0, 0.1),
     'L0_conv_b': (0.0, 0.1),
     'L0_conv_gamma': (1.0, 0.2),
     'L0_conv_beta': (0.0, 0.1),
     'L0_conv_run_mean': (0.0, 0.1),
     'L0_conv_run_var': (1.0, 0.2)}
    factors = {'L0_ffn_V_i': 4.42, 'L0_ffn_b_i': 3.268, 'L0_ffn_V_o': 3.915, 'L0_ffn_b_o': 4.885}
    for name, (base, spread) in spreads.items():
        noise = np.random.default_rng([zlib.crc32(name.encode()), seed]).standard_normal(out[name].shape)
        drawn = base * np.exp(spread * noise) if base else spread * noise
        out[name] = jnp.asarray(drawn.astype(out[name].dtype))
    for name, factor in factors.items():
        out[name] = (out[name] * factor).astype(out[name].dtype)
    return out
```

```python
from contextlib import ExitStack

import concourse.bass as bass
from concourse import mybir

F32 = mybir.dt.float32
BF16 = mybir.dt.bfloat16
ALU = mybir.AluOpType
ACT = mybir.ActivationFunctionType
AX = mybir.AxisListType

B, C, H, W = 8, 64, 16, 16
T = H * W
BQ = B // 2
COLS = BQ * T
P = 2 * C
TAPS = 9
OFF = 3 * TAPS
PW = W + 2
PADN = PW * PW
NP = 6
KG = 3
MATS = 2 * TAPS * 2
TG = 4
NG = MATS // TG
LAG = 2
RING = 3
SLOTS = 2 * W
E = 8
HID = 682
HT = -(-HID // 128)
HP = HT * 128
NCH = 4
CH = B * T // NCH
JJ = CH // 128


def build(nc, x, consts, conv_w, conv_b, sample_w, bn, lstm_u, lstm_v, lstm_b, router, w13, w2, out):
    with ExitStack() as ctx:
        def sb(name, shape, dt=F32):
            return ctx.enter_context(nc.sbuf_tensor(name, shape, dt))

        def sem(name):
            return ctx.enter_context(nc.semaphore(name))

        bank = [ctx.enter_context(nc.psum_tensor(f"bank{i}", [P, 512], F32)) for i in range(8)]

        tent_c = sb("tent_c", [P, 2, 2, TAPS, 16])
        ident = sb("ident", [P, P])
        mean_w = sb("mean_w", [P, P])
        rank_c = sb("rank_c", [P, E])
        xs = sb("xs", [P, COLS])
        xn = sb("xn", [P, COLS + T])
        xc = sb("xc", [P, COLS])
        sq = sb("sq", [P, COLS])
        pad = [sb(f"pad{p}", [P, PADN]) for p in range(2)]
        convw = [sb(f"convw{l}", [P, 2, NP, OFF]) for l in range(2)]
        convb = sb("convb", [OFF, 2])
        samw = [sb(f"samw{l}", [P, 2, TAPS * C]) for l in range(2)]
        bnp = sb("bnp", [P, 6])
        bnw = sb("bnw", [P, 6])
        om = sb("om", [OFF, T])
        omt = [sb(f"omt{p}", [P, 2, OFF]) for p in range(2)]
        sig = [sb(f"sig{p}", [P, 2, TAPS]) for p in range(2)]
        dist = sb("dist", [P, 2, 2 * TAPS, 16])
        ndist = sb("ndist", [P, 2, 2 * TAPS, 16])
        tent = [sb(f"tent{p}", [P, 2, 2 * TAPS, 16]) for p in range(2)]
        tentx = [sb(f"tentx{p}", [P, 2, TAPS, 16]) for p in range(2)]
        st = [sb(f"st{p}", [P, 2, TAPS, 256]) for p in range(2)]
        smat = sb("smat", [P, RING, TG, 128])
        zw = [sb(f"zw{p}", [P, 2, TAPS * C]) for p in range(2)]
        osb = sb("osb", [P, 2, 2, C])
        ores = sb("ores", [P, T])
        lu = sb("lu", [P, 2, 192])
        lv = sb("lv", [C, 192])
        lb = sb("lb", [1, 192])
        ones = sb("ones", [1, 128])
        hr = sb("hr", [C, SLOTS, B])
        gate_i = sb("gate_i", [C, B, 2])
        cell = sb("cell", [C, B, 2])
        tcell = sb("tcell", [C, B])
        cand = sb("cand", [C, B, 2])
        og = sb("og", [C, B])
        hup = sb("hup", [P, 2, BQ, W])
        rw = sb("rw", [P, 2 * E])
        stage = sb("stage", [P, 2, 2 * HP])
        resid = sb("resid", [P, 2 * HP])
        wa = sb("wa", [P, E, 2 * HP], BF16)
        wb = sb("wb", [P, E, 2 * HP], BF16)
        wc = sb("wc", [P, E, 2 * HP], BF16)
        w2s = sb("w2s", [P, E, HT, C])

        def over(t, at, shape, dt=F32):
            n = 1
            for s in shape[1:]:
                n *= s
            flat = t.rearrange("p a b c -> p (a b c)")
            if dt == BF16:
                return flat[:, at:at + n // 2].bitcast(BF16)
            return flat[:, at:at + n]

        epsc = sb("epsc", [P, 2])
        st0, st1 = st[0][:, :, :, :], st[1][:, :, :, :]
        r12 = over(st0, 0, [P, 2 * COLS], BF16)
        r13 = over(st0, 1024, [P, 2 * COLS], BF16)
        x1 = over(st0, 2048, [P, COLS], BF16)
        x2 = over(st0, 2560, [P, COLS], BF16)
        x3 = over(st0, 3072, [P, COLS], BF16)
        acc = over(st1, 0, [P, 1024]).rearrange("p (j h c) -> p j h c", j=8, h=2)
        silu = over(st1, 1024, [P, 1024]).rearrange("p (u n) -> p u n", u=2)
        hid = over(st1, 2048, [P, 1536]).rearrange("p (u n) -> p u n", u=3)
        gt = over(st1, 3584, [P, 1024]).rearrange("p (k g e) -> p k g e", k=8, e=E)
        spare = smat[:, :, :, :].rearrange("p a b c -> p (a b c)")
        small = spare[:, 0:128].rearrange("p (k g) -> p k g", k=8)
        g1 = spare[:, 128:256].rearrange("p (j h e) -> p j h e", j=8, h=2)
        ge = spare[:, 256:272].rearrange("p (j h) -> p j h", j=8)

        S = {}

        def s(name):
            if name not in S:
                S[name] = sem(name)
            return S[name]

        for l in range(2):
            for n in ("pad_main", "pad_shift", "conv_done", "om_sb", "omt_ps", "omt_sb", "z_ps", "z_act",
                      "z_dve", "sig", "tent", "st_ready", "tr_done", "tr_copied", "sz_done",
                      "dist", "ndist", "tents", "osb", "out_ps", "out_sb", "res"):
                s(f"c{l}_{n}")
        for l in range(4):
            for n in ("mean", "xc", "sq", "var", "sd", "rs", "xn"):
                s(f"n{l}_{n}")
        for n in ("ld_const", "ld_x", "ld_conv", "ld_lstm", "ld_w2", "zero", "bn_a", "bn_d", "g_a", "g_b", "split_up", "tick", "tick_d", "g_c", "m_ge", "m_sm", "stage_in0", "stage_in1",
                  "split", "split_done", "l_x", "l_gi", "l_o", "l_act", "l_oact", "l_c", "l_tc", "l_h", "l_hc",
                  "l_up", "l_res", "l_init", "m_parts", "m_rep", "m_log", "m_max", "m_exp", "m_g", "m_acc0",
                  "m_h", "m_silu", "m_hid", "m_y", "m_acc", "m_tr", "m_out", "st_out"):
            s(n)

        def pixels(t, p0, p1, b4):
            return t[p0:p1, bass.ts(b4, T)]

        block = ctx.enter_context(nc.Block())

        @block.sync
        def _(sp):
            sp.dma_start(xs[0:C, :].rearrange("c (b t) -> c b t", b=BQ), x[0]).then_inc(s("ld_x"), 16)
            sp.dma_start(xs[C:P, :].rearrange("c (b t) -> c b t", b=BQ), x[1]).then_inc(s("ld_x"), 16)
            sp.dma_start(mean_w[:, :], consts[:, 0:P]).then_inc(s("ld_const"), 16)
            sp.dma_start(ident[:, :], consts[:, P:2 * P]).then_inc(s("ld_const"), 16)
            sp.dma_start(rank_c[:, :], consts[:, 2 * P:2 * P + E]).then_inc(s("ld_const"), 16)
            sp.dma_start(tent_c[:, :, :, :, :].rearrange("p a b c d -> p (a b c d)"),
                         consts[:, 2 * P + E:]).then_inc(s("ld_const"), 16)
            def load_expert(e, q):
                for hf in range(2):
                    sp.dma_start(stage[hf * C:hf * C + C, q, :], w13[e]).then_inc(s(f"stage_in{q}"), 16)

            load_expert(0, 0)
            load_expert(1, 1)
            with sp.Fori(1, E // 2) as i:
                for q in range(2):
                    sp.wait_ge(s("split"), 2 * i + q - 1)
                    load_expert(2 * i + q, q)
            for q in range(2):
                sp.wait_ge(s("m_out"), q + 1)
                for hf in range(2):
                    sp.dma_start(out[hf][:, 2 * q:2 * q + 2, :],
                                 xs[hf * C:hf * C + C, q * 512:q * 512 + 512]
                                 .rearrange("c (b t) -> c b t", b=2)).then_inc(s("st_out"), 16)
            sp.wait_ge(s("st_out"), 64)

        @block.tensor
        def _(pe):
            def norm(l, ready):
                for wait_sem, v in ready:
                    pe.wait_ge(s(wait_sem), v)
                for j in range(2):
                    nc.tensor.matmul(bank[j][:, :], mean_w[:, :], xs[:, j * 512:j * 512 + 512],
                                     start=True, stop=True).then_inc(s(f"n{l}_mean"), 1)
                for j in range(2):
                    pe.wait_ge(s(f"n{l}_sq"), j + 1)
                    nc.tensor.matmul(bank[2 + j][:, :], mean_w[:, :], sq[:, j * 512:j * 512 + 512],
                                     start=True, stop=True).then_inc(s(f"n{l}_var"), 1)

            def conv(l):
                c = f"c{l}_"
                pe.sem_inc(s(c + "tr_done"), 1 + NG)
                pe.sem_inc(s(c + "sz_done"), 1)
                pe.sem_inc(s(c + "out_ps"), 1)

                def offsets(m, p):
                    pe.wait_ge(s(c + "pad_main"), 2 * m + 2)
                    pe.wait_ge(s(c + "pad_shift"), m + 1)
                    pe.wait_ge(s(c + "omt_sb"), m)
                    img = pad[p][:, :].rearrange("p (y x) -> p y x", x=PW)
                    for j in range(NP):
                        ky, kx = j // 2, 2 * (j % 2)
                        mm = nc.tensor.matmul(bank[0][0:OFF, 0:T], convw[l][:, p, j, :],
                                              img[:, ky:ky + H, kx:kx + W], start=(j == 0), stop=(j == NP - 1))
                    mm.then_inc(s(c + "conv_done"), 1)

                    def taps(half):
                        pe.wait_ge(s(c + "z_act"), 2 * m + half)
                        pe.wait_ge(s(c + "z_dve"), 2 * m + half)
                        src = sq[:, p * T + half * 128:p * T + half * 128 + 128]
                        for j in range(2):
                            mm = nc.tensor.matmul(bank[1 + j][:, 0:288], src,
                                                  samw[l][:, p, j * 288:j * 288 + 288], start=True, stop=True)
                            mm.then_inc(s(c + "z_ps"), 1)

                    taps(0)
                    pe.wait_ge(s("ld_const"), 64)
                    pe.wait_ge(s(c + "om_sb"), m + 1)
                    for t in range(2):
                        mm = nc.tensor.transpose(bank[0][:, 256 + t * OFF:256 + (t + 1) * OFF],
                                                 om[:, t * 128:t * 128 + 128], ident[0:OFF, 0:OFF])
                    mm.then_inc(s(c + "omt_ps"), 1)
                    taps(1)

                def sample(m, p):
                    for g in range(NG + LAG):
                        if g < NG:
                            last = TG * g + TG - 1
                            pe.wait_ge(s(c + "st_ready"), 1 + 6 * m + last // (2 * KG) + 1)
                            if g >= RING:
                                pe.wait_ge(s(c + "tr_copied"), 1 + NG * m + g - RING + 1)
                            else:
                                pe.wait_ge(s(c + "tr_copied"), 1 + NG * m)
                            for k in range(TG):
                                t, tap, half = (TG * g + k) // 18, (TG * g + k) % 18 // 2, k % 2
                                mm = nc.tensor.transpose(bank[3 + g % RING][:, k * 128:k * 128 + 128],
                                                         st[p][:, t, tap, half * 128:half * 128 + 128], ident[:, :])
                            mm.then_inc(s(c + "tr_done"), 1)
                        if g >= LAG:
                            h = g - LAG
                            pe.wait_ge(s(c + "tr_copied"), 1 + NG * m + h + 1)
                            if h == 0:
                                pe.wait_ge(s(c + "z_act"), 2 * m + 2)
                                pe.wait_ge(s(c + "z_dve"), 2 * m + 2)
                            for k in range(TG):
                                a = TG * h + k
                                t, tap, half = a // 18, a % 18 // 2, k % 2
                                mm = nc.tensor.matmul(bank[6][:, (2 * p + t) * C:(2 * p + t + 1) * C],
                                                      smat[:, h % RING, k, :],
                                                      zw[p][:, half, tap * C:tap * C + C],
                                                      start=(p == 0 and a == 0), stop=(a % 18 == 17),
                                                      skip_group_check=True)
                            mm.then_inc(s(c + "sz_done"), 1)

                def turn(i):
                    pe.wait_ge(s(c + "osb"), i + 1)
                    pe.wait_ge(s(c + "out_sb"), 1 + i)
                    for t in range(2):
                        mm = nc.tensor.transpose(bank[7][:, t * 128:t * 128 + 128],
                                                 osb[:, t, :, :].rearrange("p h c -> p (h c)"), ident[:, :])
                    mm.then_inc(s(c + "out_ps"), 1)

                def pair(i, last):
                    offsets(2 * i + 1, 1)
                    sample(2 * i, 0)
                    if not last:
                        offsets(2 * i + 2, 0)
                    sample(2 * i + 1, 1)
                    turn(i)

                offsets(0, 0)
                with pe.Fori(0, BQ - 1) as i:
                    pair(i, False)
                pair(BQ - 1, True)

            pe.wait_ge(s("ld_const"), 64)
            norm(0, [("ld_x", 32)])
            pe.wait_ge(s("ld_conv"), 16 * 5)
            pe.wait_ge(s("n0_xn"), 2)
            conv(0)

            norm(1, [("c0_res", 1 + BQ)])
            pe.wait_ge(s("ld_lstm"), 16 * 3)
            pe.wait_ge(s("n1_xn"), 2)
            pe.wait_ge(s("l_init"), 4)

            def gates_x(r, q, k):
                bk, lo, m = ((bank[q], 0, 128), (bank[2 + q], 128, C))[k // 3]
                if k % 3 == 0:
                    nc.tensor.matmul(bk[0:m, 0:128], lb[:, lo:lo + m], ones[:, :],
                                     start=True, stop=False, skip_group_check=True)
                else:
                    hf = k % 3 - 1
                    rhs = xn[:, bass.ds(r * W, COLS)].rearrange("p (b t) -> p b t", b=BQ)[:, :, 0:W]
                    nc.tensor.matmul(bk[0:m, hf * C:hf * C + C], lu[:, hf, lo:lo + m], rhs,
                                     start=False, stop=False, skip_group_check=True)

            for k in range(6):
                gates_x(0, 0, k)
            with pe.Fori(0, H // 2) as i:
                for q in range(2):
                    for t in range(W):
                        slot = q * W + t
                        step = pe.snap(SLOTS * i + slot + 1)
                        pe.wait_ge(s("l_h"), step)
                        prev = hr[:, (slot - 1) % SLOTS, :]
                        gi = bank[q][:, 0:128].rearrange("p (b t) -> p t b", t=W)[:, t, :]
                        go = bank[2 + q][0:C, 0:128].rearrange("p (b t) -> p t b", t=W)[:, t, :]
                        nc.tensor.matmul(gi, lv[:, 0:128], prev, start=False, stop=True,
                                         skip_group_check=True).then_inc(s("l_gi"), 1)
                        nc.tensor.matmul(go, lv[:, 128:192], prev, start=False, stop=True,
                                         skip_group_check=True).then_inc(s("l_o"), 1)
                        if 4 <= t < 10:
                            gates_x(2 * i + q + 1, 1 - q, t - 4)

            pe.wait_ge(s("ld_w2"), 48)
            norm(2, [("l_res", H + 2)])
            pe.wait_ge(s("n2_xn"), 2)
            conv(1)

            norm(3, [("c1_res", 1 + BQ)])
            pe.wait_ge(s("n3_xn"), 2)
            for j in range(8):
                mm = nc.tensor.matmul(bank[6][:, j * 16:j * 16 + 16], xn[:, j * 128:j * 128 + 128], rw[:, :],
                                      start=(j == 0), stop=True, skip_group_check=True)
            mm.then_inc(s("m_log"), 1)
            pe.wait_ge(s("m_rep"), 8)
            pe.wait_ge(s("split_done"), 1 + E)
            pe.wait_ge(s("split_up"), E)
            pe.wait_ge(s("ld_w2"), 48)
            U = NCH * HT
            with pe.Fori(0, E) as e:
                for u in range(U + 1):
                    if u < U:
                        ch, t = u // HT, u % HT
                        tok = slice(ch * CH, ch * CH + CH)
                        if u >= 2:
                            pe.wait_ge(s("m_hid"), 1 + U * e + u - 1)
                        else:
                            pe.wait_ge(s("m_hid"), 1 + U * e)
                        for k in range(2):
                            col = k * HP + t * 128
                            bk = bank[2 * k + u % 2]
                            nc.tensor.matmul(bk[:, :], wa[:, e, col:col + 128], r12[:, tok], start=True, stop=False)
                            nc.tensor.matmul(bk[:, :], wb[:, e, col:col + 128], r12[:, tok], start=False, stop=False)
                            mm = nc.tensor.matmul(bk[:, :], wc[:, e, col:col + 128], r13[:, tok],
                                                  start=False, stop=True)
                            mm.then_inc(s("m_h"), 1)
                    if u >= 1:
                        v = u - 1
                        ch, t = v // HT, v % HT
                        pe.wait_ge(s("m_hid"), 1 + U * e + v + 1)
                        if t == 0:
                            if ch >= 2:
                                pe.wait_ge(s("m_acc"), 1 + NCH * e + ch - 1)
                            else:
                                pe.wait_ge(s("m_acc"), 1 + NCH * e)
                        for j in range(JJ):
                            mm = nc.tensor.matmul(bank[4 + ch % 2][:, j * C:j * C + C],
                                                  hid[:, v % 3, j * 128:j * 128 + 128], w2s[:, e, t, :],
                                                  start=(t == 0 and j == 0), stop=(t == HT - 1),
                                                  skip_group_check=True)
                        if t == HT - 1:
                            mm.then_inc(s("m_y"), 1)
            pe.wait_ge(s("m_acc"), 1 + NCH * E)
            for j in range(8):
                mm = nc.tensor.transpose(bank[6 + j // 4][:, j % 4 * 128:j % 4 * 128 + 128],
                                         acc[:, j, :, :].rearrange("p h c -> p (h c)"), ident[:, :])
                if j % 4 == 3:
                    mm.then_inc(s("m_tr"), 1)

        @block.scalar
        def _(act):
            act.dma_start(convw[0][:, :, :, :], conv_w[0]).then_inc(s("ld_conv"), 16)
            act.dma_start(convb[:, :], conv_b).then_inc(s("ld_conv"), 16)
            act.dma_start(samw[0][:, :, :], sample_w[0]).then_inc(s("ld_conv"), 16)
            act.dma_start(bnp[:, :], bn).then_inc(s("ld_conv"), 16)
            act.dma_start(convw[1][:, :, :, :], conv_w[1]).then_inc(s("ld_conv"), 16)
            act.dma_start(samw[1][:, :, :], sample_w[1]).then_inc(s("ld_w2"), 16)
            act.dma_start(lu[:, :, :], lstm_u).then_inc(s("ld_lstm"), 16)
            act.dma_start(lv[:, :], lstm_v).then_inc(s("ld_lstm"), 16)
            act.dma_start(lb[:, :], lstm_b).then_inc(s("ld_lstm"), 16)
            act.dma_start(rw[:, :], router).then_inc(s("ld_w2"), 16)
            act.dma_start(w2s[:, :, :, :], w2).then_inc(s("ld_w2"), 16)


            def norm(l, eps):
                for j in range(2):
                    col = slice(j * 512, j * 512 + 512)
                    act.wait_ge(s(f"n{l}_xc"), j + 1)
                    nc.scalar.activation(sq[:, col], xc[:, col], ACT.Square).then_inc(s(f"n{l}_sq"), 1)
                for j in range(2):
                    col = slice(j * 512, j * 512 + 512)
                    act.wait_ge(s(f"n{l}_var"), j + 1)
                    nc.scalar.activation(sq[:, col], bank[2 + j][:, :], ACT.Sqrt,
                                         bias=epsc[:, eps:eps + 1]).then_inc(s(f"n{l}_sd"), 1)

            def conv(l):
                c = f"c{l}_"

                act.sem_inc(s(c + "tr_copied"), 1)
                act.sem_inc(s(c + "out_sb"), 1)

                def shift(m, p, b4):
                    if not (isinstance(m, int) and m == 0):
                        act.wait_ge(s(c + "z_ps"), 4 * (m - 1))
                    act.wait_ge(s(c + "pad_main"), 2 * m + 1)
                    dst = pad[p][C * (1 - p):C * (1 - p) + C, :].rearrange("c (y x) -> c y x", x=PW)
                    nc.scalar.copy(dst[:, 1:1 + H, 0:W],
                                   pixels(xn, C * p, C * p + C, b4).rearrange("c (y x) -> c y x", x=W))\
                        .then_inc(s(c + "pad_shift"), 1)

                def offsets(m, p, b4_next, more=True):
                    act.wait_ge(s(c + "conv_done"), m + 1)
                    nc.scalar.activation(om[:, :], bank[0][0:OFF, 0:T], ACT.Identity,
                                         bias=convb[:, l:l + 1]).then_inc(s(c + "om_sb"), 1)
                    act.wait_ge(s(c + "z_ps"), 4 * m + 1)
                    nc.scalar.copy(zw[p][:, 0, 0:288], bank[1][:, 0:288]).then_inc(s(c + "z_act"), 1)
                    if not (isinstance(m, int) and m == 0):
                        act.wait_ge(s(c + "tent"), 1 + m - 1)
                    act.wait_ge(s(c + "omt_ps"), m + 1)
                    nc.scalar.copy(omt[p][:, :, :].rearrange("p t k -> p (t k)"), bank[0][:, 256:256 + 2 * OFF])\
                        .then_inc(s(c + "omt_sb"), 1)
                    act.wait_ge(s(c + "z_ps"), 4 * m + 3)
                    nc.scalar.copy(zw[p][:, 1, 0:288], bank[1][:, 0:288]).then_inc(s(c + "z_act"), 1)
                    act.wait_ge(s(c + "omt_sb"), m + 1)
                    nc.scalar.activation(sig[p][:, :, :], omt[p][:, :, 2 * TAPS:OFF], ACT.Sigmoid)\
                        .then_inc(s(c + "sig"), 1)
                    if more:
                        shift(m + 1, 1 - p, b4_next)

                def copies(m, p):
                    for g in range(NG):
                        act.wait_ge(s(c + "tr_done"), 1 + NG * (m + 1) + g + 1)
                        act.wait_ge(s(c + "sz_done"), 1 + NG * m + max(g - RING + 1, 0))
                        nc.scalar.copy(smat[:, g % RING, :, :].rearrange("p k n -> p (k n)"),
                                       bank[3 + g % RING][:, :]).then_inc(s(c + "tr_copied"), 1)

                def result(i):
                    act.wait_ge(s(c + "sz_done"), 1 + NG * (2 * i + 2))
                    act.wait_ge(s(c + "out_ps"), 1 + i)
                    nc.scalar.copy(osb[:, :, :, :].rearrange("p t h c -> p h t c"),
                                   bank[6][:, 0:256].rearrange("p (h t c) -> p h t c", h=2, t=2))\
                        .then_inc(s(c + "osb"), 1)
                    act.wait_ge(s(c + "out_ps"), 1 + i + 1)
                    act.wait_ge(s(c + "res"), 1 + i)
                    if l == 0:
                        nc.scalar.activation(ores[:, :], bank[7][:, 0:T], ACT.Relu, scale=bnw[:, 2:3],
                                             bias=bnw[:, 4:5]).then_inc(s(c + "out_sb"), 1)
                    else:
                        nc.scalar.copy(ores[:, :], bank[7][:, 0:T]).then_inc(s(c + "out_sb"), 1)

                def pair(i, last):
                    offsets(2 * i + 1, 1, i + 1, not last)
                    copies(2 * i, 0)
                    if not last:
                        offsets(2 * i + 2, 0, i + 1)
                    copies(2 * i + 1, 1)
                    result(i)

                act.wait_ge(s(f"n{2 * l}_xn"), 2)
                act.wait_ge(s("zero"), 2)
                shift(0, 0, 0)
                offsets(0, 0, 0)
                with act.Fori(0, BQ - 1) as i:
                    pair(i, False)
                pair(BQ - 1, True)

            act.wait_ge(s("zero"), 4)
            norm(0, 0)
            act.wait_ge(s("ld_conv"), 16 * 5)
            nc.scalar.activation(bnw[:, 0:1], bnp[:, 3:4], ACT.Sqrt, bias=epsc[:, 1:2]).then_inc(s("bn_a"), 1)
            act.wait_ge(s("bn_d"), 5)
            conv(0)

            norm(1, 1)
            act.wait_ge(s("l_init"), 4)
            with act.Fori(0, H // 2) as i:
                for q in range(2):
                    for t in range(W):
                        slot = q * W + t
                        gates = bank[q][:, 0:128].rearrange("p (b t) -> p t b", t=W)[:, t, :]
                        gate_o = bank[2 + q][0:C, 0:128].rearrange("p (b t) -> p t b", t=W)[:, t, :]
                        step = act.snap(SLOTS * i + slot + 1)
                        act.wait_ge(s("l_gi"), step)
                        nc.scalar.activation(cand[:, :, 0], gates[0:C, :], ACT.Tanh)
                        nc.scalar.activation(gate_i[:, :, 1],
                                             gates[C:P, :], ACT.Sigmoid).then_inc(s("l_act"), 1)
                        act.wait_ge(s("l_o"), step)
                        nc.scalar.activation(og[:, :], gate_o, ACT.Sigmoid).then_inc(s("l_oact"), 1)
                        act.wait_ge(s("l_c"), step)
                        nc.scalar.activation(tcell[:, :], cell[:, :, 1], ACT.Tanh).then_inc(s("l_tc"), 1)

            norm(2, 0)
            conv(1)

            norm(3, 1)
            act.wait_ge(s("m_max"), 2)
            nc.scalar.activation(gt[:, 0, :, :], gt[:, 1, :, :], ACT.Exp).then_inc(s("m_exp"), 1)
            U = NCH * HT
            with act.Fori(0, E) as e:
                for u in range(U):
                    act.wait_ge(s("m_h"), 2 * U * e + 2 * u + 1)
                    nc.scalar.activation(silu[:, u % 2, :], bank[u % 2][:, :], ACT.Silu)\
                        .then_inc(s("m_silu"), 1)

        @block.gpsimd
        def _(gp):
            for p in range(2):
                nc.gpsimd.memset(pad[p][:, :], 0.0).then_inc(s("zero"), 1)
            nc.gpsimd.memset(epsc[:, 0:1], 1e-6).then_inc(s("zero"), 1)
            nc.gpsimd.memset(epsc[:, 1:2], 1e-5).then_inc(s("zero"), 1)

            def conv(l):
                c = f"c{l}_"

                def split(e, i, q):
                    gp.wait_ge(s(f"stage_in{q}"), 32 * (i + 1))
                    gp.sem_inc(s("tick"), 1)
                    nc.gpsimd.tensor_copy(wa[:, e, :], stage[:, q, :]).then_inc(s("g_a"), 1)
                    gp.wait_ge(s("g_a"), e + 1)
                    gp.wait_ge(s("split_done"), 1 + e)
                    gp.sem_inc(s("tick"), 1)
                    nc.gpsimd.tensor_tensor(resid[:, :], stage[:, q, :], wa[:, e, :], ALU.subtract)\
                        .then_inc(s("split"), 1)
                    gp.wait_ge(s("split"), e + 1)
                    nc.gpsimd.tensor_copy(wb[:, e, :], resid[:, :]).then_inc(s("g_b"), 1)
                    gp.wait_ge(s("g_b"), e + 1)
                    gp.sem_inc(s("tick"), 1)
                    nc.gpsimd.tensor_tensor(wc[0:C, e, :], resid[0:C, :], wb[0:C, e, :], ALU.subtract)\
                        .then_inc(s("split_done"), 1)

                def add(i):
                    gp.wait_ge(s(c + "out_sb"), 1 + i + 1)
                    gp.sem_inc(s("tick"), 1)
                    nc.gpsimd.tensor_tensor(pixels(xs, 0, P, i), pixels(xs, 0, P, i), ores[:, :], ALU.add)\
                        .then_inc(s(c + "res"), 1)

                def pair(i, last):
                    if l == 0:
                        split(2 * i, i, 0)
                        split(2 * i + 1, i, 1)
                    add(i)

                gp.sem_inc(s(c + "res"), 1)
                with gp.Fori(0, BQ - 1) as i:
                    pair(i, False)
                pair(BQ - 1, True)

            gp.sem_inc(s("split_done"), 1)
            conv(0)
            gp.sem_inc(s("l_res"), 2)
            xsv = xs[:, :].rearrange("p (b t) -> p b t", b=BQ)
            with gp.Fori(0, H // 2) as i:
                for q in range(2):
                    row = bass.ds((2 * i + q) * W, W)
                    gp.wait_ge(s("l_res"), 2 * i + q + 2)
                    gp.wait_ge(s("l_h"), SLOTS * i + (q + 1) * W + 1)
                    gp.sem_inc(s("tick"), 1)
                    for hf in range(2):
                        nc.gpsimd.tensor_copy(hup[C * hf:C * hf + C, q, :, :],
                                              hr[:, q * W:q * W + W, BQ * hf:BQ * hf + BQ].rearrange("p t b -> p b t"))\
                            .then_inc(s("l_up"), 1)
                    gp.wait_ge(s("l_up"), 2 * (2 * i + q + 1))
                    gp.sem_inc(s("tick"), 1)
                    nc.gpsimd.tensor_tensor(xsv[:, :, row], xsv[:, :, row], hup[:, q, :, :], ALU.add)\
                        .then_inc(s("l_res"), 1)
            conv(1)

        @block.vector
        def _(dve):
            def norm(l):
                for j in range(2):
                    col = slice(j * 512, j * 512 + 512)
                    dve.wait_ge(s(f"n{l}_mean"), j + 1)
                    nc.vector.tensor_tensor(xc[:, col], xs[:, col], bank[j][:, :], ALU.subtract)\
                        .then_inc(s(f"n{l}_xc"), 1)
                for j in range(2):
                    col = slice(j * 512, j * 512 + 512)
                    dve.wait_ge(s(f"n{l}_sd"), j + 1)
                    nc.vector.reciprocal(sq[:, col], sq[:, col]).then_inc(s(f"n{l}_rs"), 1)
                    dve.wait_ge(s(f"n{l}_rs"), j + 1)
                    nc.vector.tensor_tensor(xn[:, col], xc[:, col], sq[:, col], ALU.mult)\
                        .then_inc(s(f"n{l}_xn"), 1)

            def conv(l):
                c = f"c{l}_"

                def offsets(m, p):
                    dve.wait_ge(s(c + "z_ps"), 4 * m + 2)
                    nc.vector.tensor_copy(zw[p][:, 0, 288:576], bank[2][:, 0:288]).then_inc(s(c + "z_dve"), 1)
                    dve.wait_ge(s(c + "omt_sb"), m + 1)
                    shift = omt[p][:, :, 0:2 * TAPS].unsqueeze(3).broadcast_to([P, 2, 2 * TAPS, 16])
                    nc.vector.tensor_tensor(dist[:, :, :, :], tent_c[:, :, :, :, :].rearrange("p t a k n -> p t (a k) n"),
                                            shift, ALU.add).then_inc(s(c + "dist"), 1)
                    dve.wait_ge(s(c + "dist"), m + 1)
                    nc.vector.scalar_tensor_tensor(out=ndist[:, :, :, :], in0=dist[:, :, :, :], scalar=-1.0,
                                                   in1=dist[:, :, :, :], op0=ALU.mult, op1=ALU.min)\
                        .then_inc(s(c + "ndist"), 1)
                    dve.wait_ge(s(c + "ndist"), m + 1)
                    dve.wait_ge(s(c + "st_ready"), 1 + 6 * m)
                    nc.vector.tensor_scalar(tent[p][:, :, :, :], ndist[:, :, :, :], 1.0, 0.0, ALU.add, ALU.max)\
                        .then_inc(s(c + "tents"), 1)
                    dve.wait_ge(s(c + "z_ps"), 4 * m + 4)
                    nc.vector.tensor_copy(zw[p][:, 1, 288:576], bank[2][:, 0:288]).then_inc(s(c + "z_dve"), 1)
                    dve.wait_ge(s(c + "tents"), m + 1)
                    dve.wait_ge(s(c + "sig"), m + 1)
                    nc.vector.tensor_tensor(tentx[p][:, :, :, :], tent[p][:, :, TAPS:2 * TAPS, :],
                                            sig[p][:, :, :].unsqueeze(3).broadcast_to([P, 2, TAPS, 16]), ALU.mult)\
                        .then_inc(s(c + "tent"), 1)

                def image(m, p, b4):
                    if not (isinstance(m, int) and m < 2):
                        dve.wait_ge(s(c + "z_ps"), 4 * (m - 1))
                        dve.sem_inc(s("tick_d"), 1)
                    nc.vector.tensor_copy(
                        pad[p][:, :].rearrange("c (y x) -> c y x", x=PW)[:, 1:1 + H, 1:1 + W],
                        pixels(xn, 0, P, b4).rearrange("c (y x) -> c y x", x=W)).then_inc(s(c + "pad_main"), 1)
                    nc.vector.tensor_copy(sq[:, p * T:p * T + T], pixels(xn, 0, P, b4))\
                        .then_inc(s(c + "pad_main"), 1)

                def outer(m, p):
                    dve.wait_ge(s(c + "tent"), 1 + m + 1)
                    dve.wait_ge(s(c + "tr_done"), 1 + NG * m)
                    for t in range(2):
                        for k in range(0, TAPS, KG):
                            ty = tent[p][:, t, k:k + KG, :].unsqueeze(3).broadcast_to([P, KG, 16, 16])
                            tx = tentx[p][:, t, k:k + KG, :].unsqueeze(2).broadcast_to([P, KG, 16, 16])
                            nc.vector.tensor_tensor(
                                st[p][:, t, k:k + KG, :].rearrange("p k (y x) -> p k y x", x=16), ty, tx, ALU.mult)\
                                .then_inc(s(c + "st_ready"), 1)

                def upper(e):
                    dve.wait_ge(s("g_a"), e + 1)
                    nc.vector.tensor_copy(wc[C:P, e, :], wa[C:P, e, :]).then_inc(s("split_up"), 1)

                dve.sem_inc(s(c + "tent"), 1)
                dve.sem_inc(s(c + "st_ready"), 1)
                dve.wait_ge(s(f"n{2 * l}_xn"), 2)
                dve.wait_ge(s("zero"), 2)
                image(0, 0, 0)
                image(1, 1, 0)
                def batch(m, p, b4_next):
                    offsets(m, p)
                    if b4_next is not None:
                        image(m + 2, p, b4_next)
                    outer(m, p)
                    if l == 0:
                        upper(m)

                with dve.Fori(0, BQ - 1) as i:
                    for p in range(2):
                        batch(2 * i + p, p, i + 1)
                for p in range(2):
                    batch(B - 2 + p, p, None)

            norm(0)
            dve.wait_ge(s("bn_a"), 1)
            nc.vector.reciprocal(bnw[:, 1:2], bnw[:, 0:1]).then_inc(s("bn_d"), 1)
            dve.wait_ge(s("bn_d"), 1)
            nc.vector.tensor_tensor(bnw[:, 2:3], bnw[:, 1:2], bnp[:, 0:1], ALU.mult).then_inc(s("bn_d"), 1)
            nc.vector.tensor_tensor(bnw[:, 3:4], bnp[:, 4:5], bnp[:, 2:3], ALU.subtract).then_inc(s("bn_d"), 1)
            dve.wait_ge(s("bn_d"), 3)
            nc.vector.tensor_tensor(bnw[:, 5:6], bnw[:, 3:4], bnw[:, 2:3], ALU.mult).then_inc(s("bn_d"), 1)
            dve.wait_ge(s("bn_d"), 4)
            nc.vector.tensor_tensor(bnw[:, 4:5], bnw[:, 5:6], bnp[:, 1:2], ALU.add).then_inc(s("bn_d"), 1)
            dve.wait_ge(s("ld_const"), 64)
            conv(0)

            norm(1)
            nc.vector.memset(hr[:, SLOTS - 1, :], 0.0).then_inc(s("l_init"), 1)
            nc.vector.memset(gate_i[:, :, :], 0.0).then_inc(s("l_init"), 1)
            nc.vector.memset(cell[:, :, :], 0.0).then_inc(s("l_init"), 1)
            nc.vector.memset(ones[:, :], 1.0).then_inc(s("l_init"), 1)
            nc.vector.memset(xn[:, COLS:COLS + T], 0.0).then_inc(s("l_h"), 1)
            dve.wait_ge(s("l_init"), 4)
            with dve.Fori(0, H // 2) as i:
                for q in range(2):
                    dve.wait_ge(s("l_res"), 1 + 2 * i + q)
                    for t in range(W):
                        slot = q * W + t
                        step = dve.snap(SLOTS * i + slot + 1)
                        dve.wait_ge(s("l_h"), step)
                        nc.vector.tensor_tensor(cand[:, :, 1], hr[:, (slot - 1) % SLOTS, :],
                                                cell[:, :, 1], ALU.mult).then_inc(s("l_hc"), 1)
                        dve.wait_ge(s("l_act"), step)
                        dve.wait_ge(s("l_hc"), step)
                        nc.vector.tensor_tensor_scan(cell[:, :, :].rearrange("p b k -> p (b k)"),
                                                     gate_i[:, :, :].rearrange("p b k -> p (b k)"),
                                                     cand[:, :, :].rearrange("p b k -> p (b k)"), 0.0,
                                                     ALU.mult, ALU.add).then_inc(s("l_c"), 1)
                        dve.wait_ge(s("l_oact"), step)
                        dve.wait_ge(s("l_tc"), step)
                        nc.vector.tensor_tensor(hr[:, slot, :], og[:, :], tcell[:, :], ALU.mult)\
                            .then_inc(s("l_h"), 1)

            norm(2)
            conv(1)

            dve.sem_inc(s("m_hid"), 1)
            dve.sem_inc(s("m_acc"), 1)
            norm(3)
            dve.wait_ge(s("n3_xn"), 2)
            nc.vector.tensor_copy(x1, xn[:, 0:COLS]).then_inc(s("m_parts"), 1)
            dve.wait_ge(s("m_parts"), 1)
            nc.vector.tensor_tensor(xc[:, :], xn[:, 0:COLS], x1, ALU.subtract).then_inc(s("m_parts"), 1)
            dve.wait_ge(s("m_parts"), 2)
            nc.vector.tensor_copy(x2, xc[:, :]).then_inc(s("m_parts"), 1)
            dve.wait_ge(s("m_parts"), 3)
            nc.vector.tensor_tensor(x3, xc[:, :], x2, ALU.subtract).then_inc(s("m_parts"), 1)
            dve.wait_ge(s("m_parts"), 4)
            for hf in range(2):
                tok = slice(hf * COLS, hf * COLS + COLS)
                src = slice(hf * C, hf * C + C)
                for dst, lo, part in ((r12, 0, x1), (r12, C, x2), (r13, 0, x1), (r13, C, x3)):
                    nc.vector.tensor_copy(dst[lo:lo + C, tok], part[src, :]).then_inc(s("m_rep"), 1)

            def col(k):
                return gt[:, k, :, :]

            def wide(a):
                return a.unsqueeze(2).broadcast_to([P, 16, E])

            red = [small[:, k, :] for k in range(8)]
            sm = [0]

            def note(ins):
                sm[0] += 1
                ins.then_inc(s("m_sm"), 1)
                dve.wait_ge(s("m_sm"), sm[0])

            rank = rank_c[:, :].unsqueeze(1).broadcast_to([P, 16, E])
            dve.wait_ge(s("m_log"), 1)
            logits = bank[6][:, 0:128].rearrange("p (g e) -> p g e", e=E)
            nc.vector.reduce_max(red[0], logits, AX.X).then_inc(s("m_max"), 1)
            dve.wait_ge(s("m_max"), 1)
            nc.vector.tensor_tensor(col(1), logits, wide(red[0]), ALU.subtract).then_inc(s("m_max"), 1)
            dve.wait_ge(s("m_exp"), 1)
            note(nc.vector.reduce_sum(red[1], col(0), AX.X))
            note(nc.vector.reciprocal(red[2], red[1]))
            note(nc.vector.tensor_tensor(col(2), col(0), wide(red[2]), ALU.mult))
            note(nc.vector.reduce_max(red[3], col(2), AX.X))
            note(nc.vector.tensor_tensor(col(3), col(2), wide(red[3]), ALU.is_equal))
            note(nc.vector.tensor_tensor(col(4), col(3), rank, ALU.mult))
            note(nc.vector.reduce_max(red[4], col(4), AX.X))
            note(nc.vector.tensor_tensor(col(5), col(4), wide(red[4]), ALU.is_equal))
            note(nc.vector.scalar_tensor_tensor(out=col(6), in0=col(5), scalar=-2.0, in1=col(2),
                                                op0=ALU.mult, op1=ALU.add))
            note(nc.vector.reduce_max(red[5], col(6), AX.X))
            note(nc.vector.tensor_tensor(col(3), col(6), wide(red[5]), ALU.is_equal))
            note(nc.vector.tensor_tensor(col(4), col(3), rank, ALU.mult))
            note(nc.vector.reduce_max(red[4], col(4), AX.X))
            note(nc.vector.tensor_tensor(col(7), col(4), wide(red[4]), ALU.is_equal))
            note(nc.vector.scalar_tensor_tensor(out=red[6], in0=red[3], scalar=1e-9, in1=red[5],
                                                op0=ALU.add, op1=ALU.add))
            note(nc.vector.reciprocal(red[7], red[6]))
            note(nc.vector.tensor_tensor(col(5), col(5), wide(red[3]), ALU.mult))
            note(nc.vector.tensor_tensor(col(7), col(7), wide(red[5]), ALU.mult))
            note(nc.vector.tensor_tensor(col(5), col(5), col(7), ALU.add))
            note(nc.vector.tensor_tensor(g1[:, :, :, :].rearrange("p j h e -> p (j h) e"), col(5),
                                         wide(red[7]), ALU.mult))
            note(nc.vector.memset(acc, 0.0))
            U = NCH * HT
            with dve.Fori(0, E) as e:
                dve.wait_ge(s("m_acc"), 1 + NCH * e)
                nc.vector.tensor_copy(ge[:, :, :].unsqueeze(3), g1[:, :, :, bass.ds(e, 1)]).then_inc(s("m_ge"), 1)
                dve.wait_ge(s("m_ge"), e + 1)

                def gather(ch):
                    dve.wait_ge(s("m_y"), NCH * e + ch + 1)
                    dve.wait_ge(s("m_acc"), 1 + NCH * e + ch)
                    for jj in range(JJ):
                        j, hf = ch % 2 * JJ + jj, ch // 2
                        mm = nc.vector.scalar_tensor_tensor(
                            out=acc[:, j, hf, :], in0=bank[4 + ch % 2][:, jj * C:jj * C + C],
                            scalar=ge[:, j, hf:hf + 1], in1=acc[:, j, hf, :], op0=ALU.mult, op1=ALU.add)
                    mm.then_inc(s("m_acc"), 1)

                for u in range(U):
                    dve.wait_ge(s("m_silu"), U * e + u + 1)
                    dve.wait_ge(s("m_h"), 2 * U * e + 2 * u + 2)
                    nc.vector.tensor_tensor(hid[:, u % 3, :], silu[:, u % 2, :], bank[2 + u % 2][:, :],
                                            ALU.mult).then_inc(s("m_hid"), 1)
                    if u % HT == 0 and u > 0:
                        gather(u // HT - 1)
                gather(NCH - 1)
            for q in range(2):
                dve.wait_ge(s("m_tr"), q + 1)
                nc.vector.tensor_tensor(xs[:, q * 512:q * 512 + 512], xs[:, q * 512:q * 512 + 512],
                                        bank[6 + q][:, :], ALU.add).then_inc(s("m_out"), 1)


def kernel(**inputs):
    import numpy as np
    import concourse.bacc as bacc
    from concourse.bass_utils import run_bass_kernel_spmd

    a = {k: np.asarray(v) for k, v in inputs.items()}
    f = np.float32

    q = np.arange(P)
    pos = np.arange(16)
    tap = np.arange(TAPS)
    cy = 8 * np.arange(2)[None, :, None, None] + (q // W)[:, None, None, None] - 1 \
        + (tap // 3)[None, None, :, None] - pos
    cx = 0 * cy + (q % W)[:, None, None, None] - 1 + (tap % 3)[None, None, :, None] - pos
    tents = np.stack([cy, cx], 2).reshape(P, -1)
    mean = np.kron(np.eye(2), np.ones((C, C))) / C
    rank = np.tile(E - np.arange(E), (P, 1))
    consts = np.concatenate([mean, np.eye(P), rank, tents], 1).astype(f)

    def halves(t, fill):
        return np.stack([np.concatenate([t, fill], 0), np.concatenate([fill, t], 0)], 1)

    def conv_weights(w, order):
        w = w[order]
        main = np.stack([w[:, :, ky, kx] for ky in range(3) for kx in (0, 2)], 0)
        zero = np.zeros_like(w[:, :, 0, 0])
        side = np.stack([t for ky in range(3) for t in (w[:, :, ky, 1], zero)], 0)
        return halves(main.transpose(2, 0, 1), side.transpose(2, 0, 1))

    def sample_weights(w):
        t = w.transpose(1, 2, 3, 0).reshape(C, TAPS * C)
        return halves(t, np.zeros_like(t))

    split_yx = list(range(27))
    pairs_yx = list(range(0, 18, 2)) + list(range(1, 18, 2)) + list(range(18, 27))
    conv_w = np.stack([conv_weights(a["L0_conv_w_off"], split_yx), conv_weights(a["L1_conv_offset_w"], pairs_yx)])
    conv_b = np.stack([a["L0_conv_b_off"], a["L1_conv_offset_b"][pairs_yx]], 1)
    sample_w = np.stack([sample_weights(a["L0_conv_w"]), sample_weights(a["L1_conv_dcn_w"])])
    bn = np.stack([a["L0_conv_" + k] for k in ("gamma", "beta", "run_mean", "run_var", "b", "b")], 1)
    bn = np.concatenate([bn, bn], 0)
    gates = ("c", "i", "o")
    u = np.concatenate([a["L0_ffn_U_" + k] for k in gates], 1)
    lstm_u = halves(u, np.zeros_like(u))
    lstm_v = np.concatenate([a["L0_ffn_V_" + k] for k in gates], 1)
    lstm_b = np.concatenate([a["L0_ffn_b_" + k] for k in gates])[None]
    router = np.zeros((P, 2, E), f)
    router[:C, 0], router[C:, 1] = a["L1_ffn_router_w"].T, a["L1_ffn_router_w"].T
    w13 = np.zeros((E, C, 2, HP), f)
    w13[:, :, 0, :HID] = a["L1_ffn_w1"].transpose(0, 2, 1)
    w13[:, :, 1, :HID] = a["L1_ffn_w3"].transpose(0, 2, 1)
    w2 = np.zeros((E, HP, C), f)
    w2[:, :HID] = a["L1_ffn_w2"].transpose(0, 2, 1)
    w2 = w2.reshape(E, HT, 128, C).transpose(2, 0, 1, 3)

    arrays = dict(x=a["x"], consts=consts, conv_w=conv_w, conv_b=conv_b, sample_w=sample_w, bn=bn,
                  lstm_u=lstm_u, lstm_v=lstm_v, lstm_b=lstm_b, router=router.reshape(P, 2 * E),
                  w13=w13.reshape(E, C, 2 * HP), w2=w2)
    arrays = {k: np.ascontiguousarray(v) for k, v in arrays.items()}
    nc = bacc.Bacc("TRN2", target_bir_lowering=False, num_devices=1)
    dram = {k: nc.dram_tensor(k, v.shape, F32, kind="ExternalInput").ap() for k, v in arrays.items()}
    out = nc.dram_tensor("out", (B, C, H, W), F32, kind="ExternalOutput").ap()
    split = lambda t: t.rearrange("(h b) c y x -> h c b (y x)", h=2)
    build(nc, split(dram["x"]), *[dram[k] for k in list(arrays)[1:]], split(out))
    r = run_bass_kernel_spmd(nc, [arrays], core_ids=[0])
    return r.results[0]["out"]
```

```python
from contextlib import ExitStack

import concourse.bass as bass
from concourse import mybir

F32 = mybir.dt.float32
F16 = mybir.dt.float16
I32 = mybir.dt.int32
ALU = mybir.AluOpType
ACT = mybir.ActivationFunctionType
AX = mybir.AxisListType

B, C, H, W = 8, 64, 16, 16
T = H * W
BQ = B // 2
COLS = BQ * T
P = 2 * C
TAPS = 9
OFF = 3 * TAPS
PW = W + 2
PADN = PW * PW
NP = 6
KG = 3
MATS = 2 * TAPS * 2
TG = 4
NG = MATS // TG
LAG = 2
RING = 3
ROWS = 4
SLOTS = ROWS * W
E = 8
HID = 682
FT = HID // 128
REST = HID % 128
PAIRS = E // 2
PT = 2 * FT + 1
PH = PT * 128
W2B = PT + 1
MLAG = 3
MR = 4
XSCALE = 256.0
WTOP = 14
HSCALE = 2.0 ** 15 / (2 * C) ** 2
NCH = 4
CH = B * T // NCH
JJ = CH // 128


def build(nc, x, consts, conv_w, conv_b, sample_w, bn, lstm_u, lstm_v, lstm_b, router, w13, w2, out):
    with ExitStack() as ctx:
        def sb(name, shape, dt=F32):
            return ctx.enter_context(nc.sbuf_tensor(name, shape, dt))

        def sem(name):
            return ctx.enter_context(nc.semaphore(name))

        bank = [ctx.enter_context(nc.psum_tensor(f"bank{i}", [P, 512], F32)) for i in range(8)]

        tent_c = sb("tent_c", [P, 2, 2, TAPS, 16])
        ident = sb("ident", [P, P])
        mean_w = sb("mean_w", [P, P])
        rank_c = sb("rank_c", [P, E])
        xs = sb("xs", [P, COLS])
        xn = sb("xn", [P, COLS + T])
        xc = sb("xc", [P, COLS])
        sq = sb("sq", [P, COLS])
        pad = [sb(f"pad{p}", [P, PADN]) for p in range(2)]
        convw = [sb(f"convw{l}", [P, 2, NP, OFF]) for l in range(2)]
        convb = sb("convb", [OFF, 2])
        samw = [sb(f"samw{l}", [P, 2, TAPS * C]) for l in range(2)]
        bnp = sb("bnp", [P, 6])
        bnw = sb("bnw", [P, 6])
        om = sb("om", [OFF, T])
        omt = [sb(f"omt{p}", [P, 2, OFF]) for p in range(2)]
        sig = [sb(f"sig{p}", [P, 2, TAPS]) for p in range(2)]
        dist = sb("dist", [P, 2, 2 * TAPS, 16])
        ndist = sb("ndist", [P, 2, 2 * TAPS, 16])
        tent = [sb(f"tent{p}", [P, 2, 2 * TAPS, 16]) for p in range(2)]
        tentx = [sb(f"tentx{p}", [P, 2, TAPS, 16]) for p in range(2)]
        st = [sb(f"st{p}", [P, 2, TAPS, 256]) for p in range(2)]
        smat = sb("smat", [P, RING, TG, 128])
        zw = [sb(f"zw{p}", [P, 2, TAPS * C]) for p in range(2)]
        osb = sb("osb", [P, 2, 2, C])
        ores = sb("ores", [P, T])
        lu = sb("lu", [P, 2, 192])
        lv = sb("lv", [C, 192])
        lb = sb("lb", [1, 192])
        ones = sb("ones", [1, 128])
        hr = sb("hr", [C, SLOTS, B])
        gate_i = sb("gate_i", [C, B, 2])
        cell = sb("cell", [C, B, 2])
        tcell = sb("tcell", [C, B])
        cand = sb("cand", [C, B, 2])
        og = sb("og", [C, B])
        hup = sb("hup", [P, 2, BQ, W])
        rw = sb("rw", [P, 2 * E])
        wmax = sb("wmax", [P, 2])
        wpow = sb("wpow", [1, 3, 2])
        wsc = sb("wsc", [P, 8])
        w13s = sb("w13s", [P, PAIRS, 2 * PH])
        wh = [sb(f"wh{q}", [P, 2 * PH], F16) for q in range(2)]
        wl = [sb(f"wl{q}", [P, 2 * PH], F16) for q in range(2)]
        w2f = sb("w2f", [P, PAIRS, W2B, C])
        w2p = [sb(f"w2p{q}", [P, W2B, 2, C], F16) for q in range(2)]
        hid = sb("hid", [P, MR, 512])

        def over(t, at, shape, dt=F32):
            n = 1
            for s in shape[1:]:
                n *= s
            flat = t.rearrange("p a b c -> p (a b c)")
            if dt == F16:
                return flat[:, at:at + n // 2].bitcast(F16)
            return flat[:, at:at + n]

        epsc = sb("epsc", [P, 2])
        dev = sb("dev", [P, 16])
        st0, st1 = st[0][:, :, :, :], st[1][:, :, :, :]
        xp = over(st0, 0, [P, 2 * COLS], F16)
        silu = over(st0, 1024, [P, 1024]).rearrange("p (u n) -> p u n", u=2)
        acc = over(st1, 0, [P, 2048]).rearrange("p (j h n) -> p j h n", j=8, h=2)
        hh = zw[0][:, :, :].rearrange("p a b -> p (a b)")[:, 0:MR * 256].bitcast(F16) \
            .rearrange("p (u n) -> p u n", u=MR)
        hl = zw[1][:, :, :].rearrange("p a b -> p (a b)")[:, 0:MR * 256].bitcast(F16) \
            .rearrange("p (u n) -> p u n", u=MR)
        gt = xc[:, :].rearrange("p (k g e) -> p k g e", k=8, e=E)
        spare = smat[:, :, :, :].rearrange("p a b c -> p (a b c)")
        small = spare[:, 0:128].rearrange("p (k g) -> p k g", k=8)
        g1 = spare[:, 128:256].rearrange("p (j h e) -> p j h e", j=8, h=2)
        ge = spare[:, 256:320].rearrange("p (q j h k) -> p q j h k", q=2, j=8, h=2)

        S = {}

        def s(name):
            if name not in S:
                S[name] = sem(name)
            return S[name]

        for l in range(2):
            for n in ("image", "conv_done", "om_sb", "omt_ps", "omt_sb", "z_ps", "z_act",
                      "z_dve", "sig", "tent", "st_ready", "tr_done", "tr_copied", "sz_done",
                      "dist", "ndist", "tents", "osb", "out_ps", "out_sb", "res"):
                s(f"c{l}_{n}")
        for l in range(4):
            for n in ("mean", "xc", "sq", "var", "sd", "rs", "rb", "rt", "xn"):
                s(f"n{l}_{n}")
        for n in ("ld_const", "ld_mean", "ld_x", "ld_conv", "ld_lstm", "ld_w13", "ld_late", "ld_w2", "m_w0", "m_w1", "w_stored",
                  "zero", "bn_a", "bn_d", "tick", "tick_d", "tick_p", "w_max", "w_tr", "w_pow", "w_bc", "w_scale", "w_fac",
                  "w_high", "w_scaled", "l_gi", "l_o", "l_act", "l_oact", "l_c", "l_tc", "l_h", "l_hc",
                  "l_up", "l_res", "l_init", "m_high", "m_scaled", "m_parts", "m_log", "m_max", "m_exp", "m_sm", "m_ge",
                  "m_h", "m_silu", "m_hid", "m_hh", "m_hl", "m_zero", "m_sum", "m_y", "m_acc", "m_tr", "m_out", "st_out"):
            s(n)

        def pixels(t, p0, p1, b4):
            return t[p0:p1, bass.ts(b4, T)]

        block = ctx.enter_context(nc.Block())

        @block.sync
        def _(sp):
            for hf in range(2):
                sp.dma_start(xs[hf * C:hf * C + C, :].rearrange("c (b t) -> c b t", b=BQ), x[hf])\
                    .then_inc(s("ld_x"), 16)
            sp.dma_start(convw[0][:, :, :, :], conv_w[0]).then_inc(s("ld_conv"), 16)
            sp.dma_start(convb[:, :], conv_b).then_inc(s("ld_conv"), 16)
            sp.dma_start(samw[0][:, :, :], sample_w[0]).then_inc(s("ld_conv"), 16)
            sp.dma_start(bnp[:, :], bn).then_inc(s("ld_conv"), 16)
            sp.dma_start(rank_c[:, :], consts[:, 2 * P:2 * P + E]).then_inc(s("ld_const"), 16)
            sp.dma_start(tent_c[:, :, :, :, :].rearrange("p a b c d -> p (a b c d)"),
                         consts[:, 2 * P + E:]).then_inc(s("ld_const"), 16)
            sp.dma_start(convw[1][:, :, :, :], conv_w[1]).then_inc(s("ld_conv"), 16)
            sp.dma_start(samw[1][:, :, :], sample_w[1]).then_inc(s("ld_late"), 16)
            sp.dma_start(lu[:, :, :], lstm_u).then_inc(s("ld_lstm"), 16)
            sp.dma_start(lv[:, :], lstm_v).then_inc(s("ld_lstm"), 16)
            sp.dma_start(lb[:, :], lstm_b).then_inc(s("ld_lstm"), 16)
            sp.dma_start(rw[:, :], router).then_inc(s("ld_late"), 16)
            for e in range(PAIRS):
                for hf in range(2):
                    sp.dma_start(w13s[hf * C:hf * C + C, e, :], w13[e]).then_inc(s("ld_w13"), 16)
            for e in range(PAIRS):
                sp.dma_start(w2f[:, e, :, :], w2[e]).then_inc(s("ld_w2"), 16)
            def parts(q):
                kept = w13s[:, 2 + q, :].bitcast(F16).rearrange("p (k n) -> p k n", k=2)
                kept2 = w2f[:, 2 + q, :, :].rearrange("p a c -> p (a c)").bitcast(F16)
                used2 = w2p[q][:, :, :, :].rearrange("p a k c -> p (a k c)")
                return ((kept[:, 0, :], wh[q][:, :]), (kept[:, 1, :], wl[q][:, :]), (kept2, used2))

            for q in range(2):
                sp.wait_ge(s(f"m_w{q}"), 48)
                for kept, used in parts(q):
                    sp.dma_start(kept, used).then_inc(s("w_stored"), 16)
            for q in range(2):
                sp.wait_ge(s("w_stored"), 96)
                sp.wait_ge(s("m_h"), 2 * NCH * PT * (q + 1))
                sp.wait_ge(s("m_y"), NCH * (q + 1))
                for kept, used in parts(q):
                    sp.dma_start(used, kept).then_inc(s(f"m_w{q}"), 16)
            for q in range(2):
                sp.wait_ge(s("m_out"), q + 1)
                for hf in range(2):
                    sp.dma_start(out[hf][:, 2 * q:2 * q + 2, :],
                                 xs[hf * C:hf * C + C, q * 512:q * 512 + 512]
                                 .rearrange("c (b t) -> c b t", b=2)).then_inc(s("st_out"), 16)
            sp.wait_ge(s("st_out"), 64)

        @block.tensor
        def _(pe):
            def norm(l, ready):
                for wait_sem, v in ready:
                    pe.wait_ge(s(wait_sem), v)
                for j in range(2):
                    nc.tensor.matmul(bank[j][:, :], mean_w[:, :], xs[:, j * 512:j * 512 + 512],
                                     start=True, stop=True).then_inc(s(f"n{l}_mean"), 1)
                for j in range(8):
                    if j % 4 == 0:
                        pe.wait_ge(s(f"n{l}_sq"), j // 4 + 1)
                    mm = nc.tensor.matmul(bank[2][:, 2 * j:2 * j + 2], sq[:, j * 128:j * 128 + 128],
                                          mean_w[:, 0:P:C], start=(j == 0), stop=True, skip_group_check=True)
                mm.then_inc(s(f"n{l}_var"), 1)
                pe.wait_ge(s(f"n{l}_rb"), 1)
                for j in range(8):
                    mm = nc.tensor.transpose(bank[j // 4][:, j % 4 * 128:j % 4 * 128 + 128],
                                             sq[:, j * 128:j * 128 + 128], ident[:, :])
                    if j % 4 == 3:
                        mm.then_inc(s(f"n{l}_rt"), 1)

            def conv(l):
                c = f"c{l}_"
                pe.sem_inc(s(c + "tr_done"), 1 + NG)
                pe.sem_inc(s(c + "sz_done"), 1)
                pe.sem_inc(s(c + "out_ps"), 1)

                def offsets(m, p):
                    pe.wait_ge(s(c + "image"), 3 * m + 3)
                    pe.wait_ge(s(c + "omt_sb"), m)
                    img = pad[p][:, :].rearrange("p (y x) -> p y x", x=PW)
                    for j in range(NP):
                        ky, kx = j // 2, 2 * (j % 2)
                        mm = nc.tensor.matmul(bank[0][0:OFF, 0:T], convw[l][:, p, j, :],
                                              img[:, ky:ky + H, kx:kx + W], start=(j == 0), stop=(j == NP - 1))
                    mm.then_inc(s(c + "conv_done"), 1)

                def turn_offsets(m):
                    pe.wait_ge(s(c + "om_sb"), m + 1)
                    pe.sem_inc(s("tick_p"), 1)
                    for t in range(2):
                        mm = nc.tensor.transpose(bank[0][:, 256 + t * OFF:256 + (t + 1) * OFF],
                                                 om[:, t * 128:t * 128 + 128], ident[0:OFF, 0:OFF])
                    mm.then_inc(s(c + "omt_ps"), 1)

                def taps(m, p, half):
                    pe.wait_ge(s(c + "z_act"), 2 * m + half)
                    pe.wait_ge(s(c + "z_dve"), 2 * m + half)
                    src = sq[:, p * T + half * 128:p * T + half * 128 + 128]
                    for j in range(2):
                        nc.tensor.matmul(bank[1 + j][:, 0:288], src,
                                         samw[l][:, p, j * 288:j * 288 + 288], start=True, stop=True)\
                            .then_inc(s(c + "z_ps"), 1)

                def turn_weights(m, p, g):
                    last = TG * g + TG - 1
                    pe.wait_ge(s(c + "st_ready"), 1 + 6 * m + last // (2 * KG) + 1)
                    if g >= RING - 1 or not (isinstance(m, int) and m == 0):
                        pe.wait_ge(s(c + "tr_copied"), NG * m + g - RING + 2)
                    for k in range(TG):
                        t, tap, half = (TG * g + k) // 18, (TG * g + k) % 18 // 2, k % 2
                        mm = nc.tensor.transpose(bank[3 + g % RING][:, k * 128:k * 128 + 128],
                                                 st[p][:, t, tap, half * 128:half * 128 + 128], ident[:, :])
                    mm.then_inc(s(c + "tr_done"), 1)

                def sums(m, p, h):
                    pe.wait_ge(s(c + "tr_copied"), 1 + NG * m + h + 1)
                    if h == 0:
                        pe.wait_ge(s(c + "z_act"), 2 * m + 2)
                        pe.wait_ge(s(c + "z_dve"), 2 * m + 2)
                    for k in range(TG):
                        a = TG * h + k
                        t, tap, half = a // 18, a % 18 // 2, k % 2
                        mm = nc.tensor.matmul(bank[6][:, (2 * p + t) * C:(2 * p + t + 1) * C],
                                              smat[:, h % RING, k, :],
                                              zw[p][:, half, tap * C:tap * C + C],
                                              start=(p == 0 and a == 0), stop=(a % 18 == 17),
                                              skip_group_check=True)
                    mm.then_inc(s(c + "sz_done"), 1)

                def turn(i):
                    pe.wait_ge(s(c + "osb"), i + 1)
                    pe.wait_ge(s(c + "out_sb"), 1 + i)
                    for t in range(2):
                        mm = nc.tensor.transpose(bank[7][:, t * 128:t * 128 + 128],
                                                 osb[:, t, :, :].rearrange("p h c -> p (h c)"), ident[:, :])
                    mm.then_inc(s(c + "out_ps"), 1)

                def stream(m, p, ended=None, first=False, last=False):
                    for g in range(NG):
                        if g == LAG and not last:
                            offsets(m + 1, 1 - p)
                        if g == LAG + 1 and not last:
                            taps(m + 1, 1 - p, 0)
                            turn_offsets(m + 1)
                        if g == LAG + 2 and not last:
                            taps(m + 1, 1 - p, 1)
                        if g == LAG + 2 and ended is not None:
                            turn(ended)
                        turn_weights(m, p, g)
                        if g >= LAG:
                            if g == LAG and ended is not None:
                                pe.wait_ge(s(c + "osb"), ended + 1)
                            sums(m, p, g - LAG)
                        elif not first:
                            sums(m - 1, 1 - p, NG - LAG + g)

                offsets(0, 0)
                taps(0, 0, 0)
                turn_offsets(0)
                taps(0, 0, 1)
                stream(0, 0, first=True)
                with pe.Fori(0, BQ - 1) as i:
                    stream(2 * i + 1, 1)
                    stream(2 * i + 2, 0, ended=i)
                stream(B - 1, 1, last=True)
                for h in range(NG - LAG, NG):
                    sums(B - 1, 1, h)
                turn(BQ - 1)

            pe.wait_ge(s("ld_mean"), 32)
            norm(0, [("ld_x", 32)])
            pe.wait_ge(s("ld_conv"), 16 * 5)
            pe.wait_ge(s("n0_xn"), 2)
            conv(0)

            norm(1, [("c0_res", 1 + BQ)])
            pe.wait_ge(s("ld_lstm"), 16 * 3)
            pe.wait_ge(s("n1_xn"), 2)
            pe.wait_ge(s("w_max"), 2)
            for k in range(2):
                nc.tensor.transpose(bank[4][0:1, k * 128:k * 128 + 128], wmax[:, k:k + 1], ident[:, :])\
                    .then_inc(s("w_tr"), 1)
            pe.wait_ge(s("l_init"), 4)

            def gates_x(r, q, k):
                bk, lo, m = ((bank[q], 0, 128), (bank[2 + q], 128, C))[k // 3]
                if k % 3 == 0:
                    nc.tensor.matmul(bk[0:m, 0:128], lb[:, lo:lo + m], ones[:, :],
                                     start=True, stop=False, skip_group_check=True)
                else:
                    hf = k % 3 - 1
                    rhs = xn[:, bass.ds(r * W, COLS)].rearrange("p (b t) -> p b t", b=BQ)[:, :, 0:W]
                    nc.tensor.matmul(bk[0:m, hf * C:hf * C + C], lu[:, hf, lo:lo + m], rhs,
                                     start=False, stop=False, skip_group_check=True)

            for k in range(6):
                gates_x(0, 0, k)
            pe.wait_ge(s("w_pow"), 3)
            nc.tensor.matmul(bank[5][:, 0:2], ones[:, :], wpow[:, 2, :], start=True, stop=True)\
                .then_inc(s("w_bc"), 1)
            with pe.Fori(0, H // ROWS) as i:
                for q in range(ROWS):
                    for t in range(W):
                        slot = q * W + t
                        step = pe.snap(SLOTS * i + slot + 1)
                        pe.wait_ge(s("l_h"), step)
                        prev = hr[:, (slot - 1) % SLOTS, :]
                        gi = bank[q % 2][:, 0:128].rearrange("p (b t) -> p t b", t=W)[:, t, :]
                        go = bank[2 + q % 2][0:C, 0:128].rearrange("p (b t) -> p t b", t=W)[:, t, :]
                        nc.tensor.matmul(gi, lv[:, 0:128], prev, start=False, stop=True,
                                         skip_group_check=True).then_inc(s("l_gi"), 1)
                        nc.tensor.matmul(go, lv[:, 128:192], prev, start=False, stop=True,
                                         skip_group_check=True).then_inc(s("l_o"), 1)
                        if 4 <= t < 10:
                            gates_x(ROWS * i + q + 1, 1 - q % 2, t - 4)

            pe.wait_ge(s("ld_late"), 32)
            norm(2, [("l_res", H + ROWS)])
            pe.wait_ge(s("n2_xn"), 2)
            conv(1)

            norm(3, [("c1_res", 1 + BQ)])
            for j in range(8):
                if j % 4 == 0:
                    pe.wait_ge(s("n3_xn"), j // 4 + 1)
                mm = nc.tensor.matmul(bank[6][:, j * 16:j * 16 + 16], xn[:, j * 128:j * 128 + 128], rw[:, :],
                                      start=(j == 0), stop=True, skip_group_check=True)
            mm.then_inc(s("m_log"), 1)
            pe.wait_ge(s("m_parts"), 2)
            U = 2 * NCH * PT
            with pe.Fori(0, PAIRS // 2) as i:
                def first(u):
                    q, ch, k0 = u // (NCH * PT), u // PT % NCH, u % PT * 128
                    tok = slice(ch * CH, ch * CH + CH)
                    if u % (NCH * PT) == 0:
                        pe.wait_ge(s(f"m_w{q}"), 48 * i + 96)
                    pe.wait_ge(s("m_hid"), U * i + u + 1)
                    for k in range(2):
                        col = k * PH + k0
                        bk = bank[2 * k + u % 2]
                        nc.tensor.matmul(bk[:, :], wh[q][:, col:col + 128], xp[:, tok], start=True, stop=False)
                        nc.tensor.matmul(bk[:, :], wl[q][:, col:col + 128], xp[:, tok], start=False, stop=True)\
                            .then_inc(s("m_h"), 1)

                def second(u):
                    q, g, t = u // (NCH * PT), u // PT, u % PT
                    if t == 0:
                        pe.wait_ge(s("m_acc"), 4 * NCH * i + 2 * g + 2)
                    pe.wait_ge(s("m_hl"), U * i + u + 1)
                    k, n = (t // FT, 2 * C) if t < 2 * FT else (0, 4 * C)
                    rhs = w2p[q][:, t:t + n // (2 * C), :, :].rearrange("p a k c -> p (a k c)")
                    for j in range(JJ):
                        lo = j % 2 * 4 * C + k * 2 * C
                        for part in (hh, hl):
                            mm = nc.tensor.matmul(bank[4 + 2 * (g % 2) + j // 2][:, lo:lo + n],
                                                  part[:, u % MR, j * 128:j * 128 + 128], rhs,
                                                  start=(t == 0 and j % 2 == 0 and part is hh),
                                                  stop=(t == PT - 1), skip_group_check=True)
                    if t == PT - 1:
                        mm.then_inc(s("m_y"), 1)

                for u in range(U + MLAG):
                    if u < U:
                        first(u)
                    if u >= MLAG:
                        second(u - MLAG)
            for j in range(8):
                if j % 4 == 0:
                    pe.wait_ge(s("m_sum"), j // 4 + 1)
                mm = nc.tensor.transpose(bank[6 + j // 4][:, j % 4 * 128:j % 4 * 128 + 128],
                                         sq[:, j * 128:j * 128 + 128], ident[:, :])
                if j % 4 == 3:
                    mm.then_inc(s("m_tr"), 1)

        @block.scalar
        def _(act):
            act.dma_start(mean_w[:, :], consts[:, 0:P]).then_inc(s("ld_mean"), 16)
            act.dma_start(ident[:, :], consts[:, P:2 * P]).then_inc(s("ld_mean"), 16)

            def norm(l, eps):
                for j in range(2):
                    col = slice(j * 512, j * 512 + 512)
                    act.wait_ge(s(f"n{l}_xc"), j + 1)
                    nc.scalar.activation(sq[:, col], xc[:, col], ACT.Square).then_inc(s(f"n{l}_sq"), 1)
                act.wait_ge(s(f"n{l}_var"), 1)
                nc.scalar.activation(dev[:, :], bank[2][:, 0:16], ACT.Sqrt, bias=epsc[:, eps:eps + 1])\
                    .then_inc(s(f"n{l}_sd"), 1)

            def conv(l):
                c = f"c{l}_"

                act.sem_inc(s(c + "tr_copied"), 1)
                act.sem_inc(s(c + "out_sb"), 1)

                def offsets(m):
                    act.wait_ge(s(c + "conv_done"), m + 1)
                    nc.scalar.activation(om[:, :], bank[0][0:OFF, 0:T], ACT.Identity,
                                         bias=convb[:, l:l + 1]).then_inc(s(c + "om_sb"), 1)

                def taps(m, p, half):
                    act.wait_ge(s(c + "z_ps"), 4 * m + 2 * half + 1)
                    nc.scalar.copy(zw[p][:, half, 0:288], bank[1][:, 0:288]).then_inc(s(c + "z_act"), 1)

                def turned(m, p):
                    if not (isinstance(m, int) and m == 0):
                        act.wait_ge(s(c + "tent"), 1 + m - 1)
                    act.wait_ge(s(c + "omt_ps"), m + 1)
                    nc.scalar.copy(omt[p][:, :, :].rearrange("p t k -> p (t k)"), bank[0][:, 256:256 + 2 * OFF])\
                        .then_inc(s(c + "omt_sb"), 1)
                    act.wait_ge(s(c + "omt_sb"), m + 1)
                    nc.scalar.activation(sig[p][:, :, :], omt[p][:, :, 2 * TAPS:OFF], ACT.Sigmoid)\
                        .then_inc(s(c + "sig"), 1)

                def copy(m, g):
                    act.wait_ge(s(c + "tr_done"), 1 + NG * (m + 1) + g + 1)
                    if g >= RING - 1 or not (isinstance(m, int) and m == 0):
                        act.wait_ge(s(c + "sz_done"), NG * m + g - RING + 2)
                    nc.scalar.copy(smat[:, g % RING, :, :].rearrange("p k n -> p (k n)"),
                                   bank[3 + g % RING][:, :]).then_inc(s(c + "tr_copied"), 1)

                def summed(i):
                    act.wait_ge(s(c + "sz_done"), 1 + NG * (2 * i + 2))
                    act.wait_ge(s(c + "out_ps"), 1 + i)
                    nc.scalar.copy(osb[:, :, :, :].rearrange("p t h c -> p h t c"),
                                   bank[6][:, 0:256].rearrange("p (h t c) -> p h t c", h=2, t=2))\
                        .then_inc(s(c + "osb"), 1)

                def result(i):
                    act.wait_ge(s(c + "out_ps"), 1 + i + 1)
                    act.wait_ge(s(c + "res"), 1 + i)
                    if l == 0:
                        nc.scalar.activation(ores[:, :], bank[7][:, 0:T], ACT.Relu, scale=bnw[:, 2:3],
                                             bias=bnw[:, 4:5]).then_inc(s(c + "out_sb"), 1)
                    else:
                        nc.scalar.copy(ores[:, :], bank[7][:, 0:T]).then_inc(s(c + "out_sb"), 1)

                def stream(m, p, ended=None, last=False):
                    for g in range(NG):
                        if g == LAG:
                            if ended is not None:
                                summed(ended)
                            if not last:
                                offsets(m + 1)
                        if g == LAG + 1 and not last:
                            taps(m + 1, 1 - p, 0)
                            turned(m + 1, 1 - p)
                        if g == LAG + 2 and not last:
                            taps(m + 1, 1 - p, 1)
                        if g == LAG + 3 and ended is not None:
                            result(ended)
                        copy(m, g)

                offsets(0)
                taps(0, 0, 0)
                turned(0, 0)
                taps(0, 0, 1)
                stream(0, 0)
                with act.Fori(0, BQ - 1) as i:
                    stream(2 * i + 1, 1)
                    stream(2 * i + 2, 0, ended=i)
                stream(B - 1, 1, last=True)
                summed(BQ - 1)
                result(BQ - 1)

            act.wait_ge(s("zero"), 4)
            norm(0, 0)
            act.wait_ge(s("ld_conv"), 16 * 5)
            nc.scalar.activation(bnw[:, 0:1], bnp[:, 3:4], ACT.Sqrt, bias=epsc[:, 1:2]).then_inc(s("bn_a"), 1)
            act.wait_ge(s("bn_d"), 5)
            conv(0)

            norm(1, 1)
            act.wait_ge(s("l_init"), 4)
            with act.Fori(0, H // ROWS) as i:
                for q in range(ROWS):
                    for t in range(W):
                        slot = q * W + t
                        gates = bank[q % 2][:, 0:128].rearrange("p (b t) -> p t b", t=W)[:, t, :]
                        gate_o = bank[2 + q % 2][0:C, 0:128].rearrange("p (b t) -> p t b", t=W)[:, t, :]
                        step = act.snap(SLOTS * i + slot + 1)
                        act.wait_ge(s("l_gi"), step)
                        nc.scalar.activation(gate_i[:, :, 1], gates[C:P, :], ACT.Sigmoid)
                        nc.scalar.activation(cand[:, :, 0], gates[0:C, :], ACT.Tanh).then_inc(s("l_act"), 1)
                        act.wait_ge(s("l_o"), step)
                        nc.scalar.activation(og[:, :], gate_o, ACT.Sigmoid).then_inc(s("l_oact"), 1)
                        act.wait_ge(s("l_c"), step)
                        nc.scalar.activation(tcell[:, :], cell[:, :, 1], ACT.Tanh).then_inc(s("l_tc"), 1)

            norm(2, 0)
            conv(1)

            norm(3, 1)
            act.wait_ge(s("n3_xn"), 2)
            for hf in range(2):
                nc.scalar.activation(xp[hf * C:hf * C + C, hf * COLS:hf * COLS + COLS],
                                     xn[hf * C:hf * C + C, 0:COLS], ACT.Copy, scale=XSCALE)\
                    .then_inc(s("m_high"), 1)
            nc.scalar.activation(sq[:, :], xn[:, 0:COLS], ACT.Copy, scale=XSCALE).then_inc(s("m_scaled"), 1)
            act.wait_ge(s("m_max"), 2)
            nc.scalar.activation(gt[:, 0, :, :], gt[:, 1, :, :], ACT.Exp).then_inc(s("m_exp"), 1)
            U = 2 * NCH * PT
            with act.Fori(0, PAIRS // 2) as i:
                def high(u):
                    act.wait_ge(s("m_hid"), U * i + u + 3)
                    nc.scalar.copy(hh[:, u % MR, :], hid[:, u % MR, :]).then_inc(s("m_hh"), 1)

                for u in range(U):
                    act.wait_ge(s("m_h"), 2 * U * i + 2 * u + 1)
                    nc.scalar.activation(silu[:, u % 2, :], bank[u % 2][:, :], ACT.Silu, scale=wsc[:, 4:5])\
                        .then_inc(s("m_silu"), 1)
                    if u > 0:
                        high(u - 1)
                high(U - 1)

        @block.gpsimd
        def _(gp):
            for p in range(2):
                nc.gpsimd.memset(pad[p][:, :], 0.0).then_inc(s("zero"), 1)
            nc.gpsimd.memset(epsc[:, 0:1], 1e-6).then_inc(s("zero"), 1)
            nc.gpsimd.memset(epsc[:, 1:2], 1e-5).then_inc(s("zero"), 1)

            def conv(l):
                c = f"c{l}_"

                def add(i):
                    gp.wait_ge(s(c + "out_sb"), 1 + i + 1)
                    gp.sem_inc(s("tick"), 1)
                    nc.gpsimd.tensor_tensor(pixels(xs, 0, P, i), pixels(xs, 0, P, i), ores[:, :], ALU.add)\
                        .then_inc(s(c + "res"), 1)

                gp.sem_inc(s(c + "res"), 1)
                with gp.Fori(0, BQ) as i:
                    add(i)

            def split(q, n, full, high, low, scale):
                nc.gpsimd.tensor_tensor(high, full, scale, ALU.mult).then_inc(s("w_high"), 1)
                gp.wait_ge(s("w_high"), n)
                nc.gpsimd.tensor_tensor(full, full, scale, ALU.mult).then_inc(s("w_scaled"), 1)
                gp.wait_ge(s("w_scaled"), n)
                nc.gpsimd.tensor_tensor(low, full, high, ALU.subtract).then_inc(s(f"m_w{q}"), 24)

            def split_pair(e, q, n):
                split(q, n, w13s[:, e, :], wh[q][:, :], wl[q][:, :], wsc[:, 0:1].broadcast_to([P, 2 * PH]))
                split(q, n + 1, w2f[:, e, :, :], w2p[q][:, :, 0, :], w2p[q][:, :, 1, :],
                      wsc[:, 1:2].unsqueeze(2).broadcast_to([P, W2B, C]))

            conv(0)
            gp.sem_inc(s("l_res"), ROWS)
            gp.wait_ge(s("w_scale"), 2)
            gp.wait_ge(s("ld_w2"), 16 * PAIRS)
            for q in range(2):
                split_pair(2 + q, q, 2 * q + 1)
            gp.wait_ge(s("m_w1"), 48)
            xsv = xs[:, :].rearrange("p (b t) -> p b t", b=BQ)
            with gp.Fori(0, H // ROWS) as i:
                for q in range(ROWS):
                    row = bass.ds((ROWS * i + q) * W, W)
                    gp.wait_ge(s("l_res"), ROWS * i + q + ROWS)
                    gp.wait_ge(s("l_h"), SLOTS * i + (q + 1) * W + 1)
                    gp.sem_inc(s("tick"), 1)
                    for hf in range(2):
                        nc.gpsimd.tensor_copy(hup[C * hf:C * hf + C, q % 2, :, :],
                                              hr[:, q * W:q * W + W, BQ * hf:BQ * hf + BQ].rearrange("p t b -> p b t"))\
                            .then_inc(s("l_up"), 1)
                    gp.wait_ge(s("l_up"), 2 * (ROWS * i + q + 1))
                    gp.sem_inc(s("tick"), 1)
                    nc.gpsimd.tensor_tensor(xsv[:, :, row], xsv[:, :, row], hup[:, q % 2, :, :], ALU.add)\
                        .then_inc(s("l_res"), 1)
            gp.wait_ge(s("w_stored"), 96)
            for q in range(2):
                split_pair(q, q, 2 * q + 5)
            conv(1)
            gp.wait_ge(s("c1_out_ps"), 1 + BQ)
            nc.gpsimd.memset(acc, 0.0).then_inc(s("m_zero"), 1)
            gp.wait_ge(s("m_zero"), 1)
            for hf in range(2):
                src, dst = slice(hf * C, hf * C + C), slice(C - hf * C, 2 * C - hf * C)
                tok = slice(hf * COLS, hf * COLS + COLS)
                gp.wait_ge(s("m_high"), hf + 1)
                gp.wait_ge(s("m_scaled"), 1)
                if hf:
                    gp.wait_ge(s("m_parts"), hf)
                nc.gpsimd.tensor_tensor(xp[dst, tok], sq[src, :], xp[src, tok], ALU.subtract)\
                    .then_inc(s("m_parts"), 1)
            gp.wait_ge(s("m_parts"), 2)
            U = 2 * NCH * PT
            with gp.Fori(0, PAIRS // 2) as i:
                for u in range(U):
                    gp.wait_ge(s("m_hh"), U * i + u + 1)
                    nc.gpsimd.tensor_tensor(hl[:, u % MR, :], hid[:, u % MR, :], hh[:, u % MR, :], ALU.subtract)\
                        .then_inc(s("m_hl"), 1)

        @block.vector
        def _(dve):
            def norm(l):
                for j in range(2):
                    col = slice(j * 512, j * 512 + 512)
                    dve.wait_ge(s(f"n{l}_mean"), j + 1)
                    nc.vector.tensor_tensor(xc[:, col], xs[:, col], bank[j][:, :], ALU.subtract)\
                        .then_inc(s(f"n{l}_xc"), 1)
                dve.wait_ge(s(f"n{l}_sd"), 1)
                nc.vector.reciprocal(dev[:, :], dev[:, :]).then_inc(s(f"n{l}_rs"), 1)
                dve.wait_ge(s(f"n{l}_rs"), 1)
                nc.vector.tensor_copy(sq[:, :].rearrange("p (k c) -> p k c", c=C),
                                      dev[:, :].unsqueeze(2).broadcast_to([P, 16, C])).then_inc(s(f"n{l}_rb"), 1)
                for j in range(2):
                    col = slice(j * 512, j * 512 + 512)
                    dve.wait_ge(s(f"n{l}_rt"), j + 1)
                    nc.vector.tensor_tensor(xn[:, col], xc[:, col], bank[j][:, :], ALU.mult)\
                        .then_inc(s(f"n{l}_xn"), 1)

            def conv(l):
                c = f"c{l}_"

                def offsets(m, p):
                    dve.wait_ge(s(c + "z_ps"), 4 * m + 2)
                    nc.vector.tensor_copy(zw[p][:, 0, 288:576], bank[2][:, 0:288]).then_inc(s(c + "z_dve"), 1)
                    dve.wait_ge(s(c + "omt_sb"), m + 1)
                    shift = omt[p][:, :, 0:2 * TAPS].unsqueeze(3).broadcast_to([P, 2, 2 * TAPS, 16])
                    nc.vector.tensor_tensor(dist[:, :, :, :], tent_c[:, :, :, :, :].rearrange("p t a k n -> p t (a k) n"),
                                            shift, ALU.add).then_inc(s(c + "dist"), 1)
                    dve.wait_ge(s(c + "dist"), m + 1)
                    nc.vector.scalar_tensor_tensor(out=ndist[:, :, :, :], in0=dist[:, :, :, :], scalar=-1.0,
                                                   in1=dist[:, :, :, :], op0=ALU.mult, op1=ALU.min)\
                        .then_inc(s(c + "ndist"), 1)
                    dve.wait_ge(s(c + "ndist"), m + 1)
                    dve.wait_ge(s(c + "st_ready"), 1 + 6 * m)
                    nc.vector.tensor_scalar(tent[p][:, :, :, :], ndist[:, :, :, :], 1.0, 0.0, ALU.add, ALU.max)\
                        .then_inc(s(c + "tents"), 1)
                    dve.wait_ge(s(c + "z_ps"), 4 * m + 4)
                    nc.vector.tensor_copy(zw[p][:, 1, 288:576], bank[2][:, 0:288]).then_inc(s(c + "z_dve"), 1)
                    dve.wait_ge(s(c + "tents"), m + 1)
                    dve.wait_ge(s(c + "sig"), m + 1)
                    nc.vector.tensor_tensor(tentx[p][:, :, :, :], tent[p][:, :, TAPS:2 * TAPS, :],
                                            sig[p][:, :, :].unsqueeze(3).broadcast_to([P, 2, TAPS, 16]), ALU.mult)\
                        .then_inc(s(c + "tent"), 1)

                def image(m, p, b4):
                    if not (isinstance(m, int) and m < 2):
                        dve.wait_ge(s(c + "z_ps"), 4 * (m - 1))
                        dve.sem_inc(s("tick_d"), 1)
                    own, other = C * p, C * (1 - p)
                    src = pixels(xn, own, own + C, b4).rearrange("c (y x) -> c y x", x=W)
                    for lo, x0 in ((own, 1), (other, 0)):
                        dst = pad[p][lo:lo + C, :].rearrange("c (y x) -> c y x", x=PW)
                        nc.vector.tensor_copy(dst[:, 1:1 + H, x0:x0 + W], src).then_inc(s(c + "image"), 1)
                    nc.vector.tensor_copy(sq[:, p * T:p * T + T], pixels(xn, 0, P, b4))\
                        .then_inc(s(c + "image"), 1)

                def outer(m, p):
                    dve.wait_ge(s(c + "tent"), 1 + m + 1)
                    dve.wait_ge(s(c + "tr_done"), 1 + NG * m)
                    for t in range(2):
                        for k in range(0, TAPS, KG):
                            ty = tent[p][:, t, k:k + KG, :].unsqueeze(3).broadcast_to([P, KG, 16, 16])
                            tx = tentx[p][:, t, k:k + KG, :].unsqueeze(2).broadcast_to([P, KG, 16, 16])
                            nc.vector.tensor_tensor(
                                st[p][:, t, k:k + KG, :].rearrange("p k (y x) -> p k y x", x=16), ty, tx, ALU.mult)\
                                .then_inc(s(c + "st_ready"), 1)

                dve.sem_inc(s(c + "tent"), 1)
                dve.sem_inc(s(c + "st_ready"), 1)
                dve.wait_ge(s(f"n{2 * l}_xn"), 2)
                dve.wait_ge(s("zero"), 2)
                image(0, 0, 0)
                image(1, 1, 0)
                def batch(m, p, b4_next):
                    offsets(m, p)
                    outer(m, p)
                    if b4_next is not None:
                        image(m + 2, p, b4_next)

                with dve.Fori(0, BQ - 1) as i:
                    for p in range(2):
                        batch(2 * i + p, p, i + 1)
                for p in range(2):
                    batch(B - 2 + p, p, None)

            norm(0)
            dve.wait_ge(s("bn_a"), 1)
            nc.vector.reciprocal(bnw[:, 1:2], bnw[:, 0:1]).then_inc(s("bn_d"), 1)
            dve.wait_ge(s("bn_d"), 1)
            nc.vector.tensor_tensor(bnw[:, 2:3], bnw[:, 1:2], bnp[:, 0:1], ALU.mult).then_inc(s("bn_d"), 1)
            nc.vector.tensor_tensor(bnw[:, 3:4], bnp[:, 4:5], bnp[:, 2:3], ALU.subtract).then_inc(s("bn_d"), 1)
            dve.wait_ge(s("bn_d"), 3)
            nc.vector.tensor_tensor(bnw[:, 5:6], bnw[:, 3:4], bnw[:, 2:3], ALU.mult).then_inc(s("bn_d"), 1)
            dve.wait_ge(s("bn_d"), 4)
            nc.vector.tensor_tensor(bnw[:, 4:5], bnw[:, 5:6], bnp[:, 1:2], ALU.add).then_inc(s("bn_d"), 1)
            dve.wait_ge(s("ld_const"), 32)
            conv(0)
            dve.wait_ge(s("ld_w13"), 16 * 2 * PAIRS)
            nc.vector.tensor_reduce(wmax[:, 0:1], w13s[:, :, :].rearrange("p e n -> p (e n)"), AX.X, ALU.max,
                                    apply_absolute_value=True).then_inc(s("w_max"), 1)
            dve.wait_ge(s("ld_w2"), 16 * PAIRS)
            nc.vector.tensor_reduce(wmax[:, 1:2], w2f[:, :, :, :].rearrange("p e a c -> p (e a c)"), AX.X, ALU.max,
                                    apply_absolute_value=True).then_inc(s("w_max"), 1)

            norm(1)
            nc.vector.memset(hr[:, SLOTS - 1, :], 0.0).then_inc(s("l_init"), 1)
            nc.vector.memset(gate_i[:, :, :], 0.0).then_inc(s("l_init"), 1)
            nc.vector.memset(cell[:, :, :], 0.0).then_inc(s("l_init"), 1)
            nc.vector.memset(ones[:, :], 1.0).then_inc(s("l_init"), 1)
            nc.vector.memset(xn[:, COLS:COLS + T], 0.0).then_inc(s("l_h"), 1)
            dve.wait_ge(s("w_tr"), 2)
            nc.vector.reduce_max(wpow[:, 0, :], bank[4][0:1, 0:256].rearrange("p (k n) -> p k n", k=2), AX.X)\
                .then_inc(s("w_pow"), 1)
            dve.wait_ge(s("w_pow"), 1)
            nc.vector.tensor_scalar(wpow[:, 1, :], wpow[:, 0, :], 2.0 ** -100, 2.0 ** -WTOP, ALU.max, ALU.mult)\
                .then_inc(s("w_pow"), 1)
            dve.wait_ge(s("w_pow"), 2)
            nc.vector.tensor_scalar(wpow[:, 2, :].bitcast(I32), wpow[:, 1, :].bitcast(I32), 0x7F800000, None,
                                    ALU.bitwise_and).then_inc(s("w_pow"), 1)
            dve.wait_ge(s("w_bc"), 1)
            nc.vector.reciprocal(wsc[:, 0:2], bank[5][:, 0:2]).then_inc(s("w_scale"), 1)
            nc.vector.tensor_copy(wsc[:, 2:4], bank[5][:, 0:2]).then_inc(s("w_scale"), 1)
            dve.wait_ge(s("w_scale"), 2)
            nc.vector.tensor_scalar(wsc[:, 4:5], wsc[:, 2:3], 1 / XSCALE, None, ALU.mult).then_inc(s("w_fac"), 1)
            nc.vector.tensor_scalar(wsc[:, 5:6], wsc[:, 0:1], HSCALE / XSCALE / 4.0 ** WTOP, None, ALU.mult)\
                .then_inc(s("w_fac"), 1)
            nc.vector.scalar_tensor_tensor(out=wsc[:, 6:7], in0=wsc[:, 2:3], scalar=4.0 ** WTOP / HSCALE,
                                           in1=wsc[:, 2:3], op0=ALU.mult, op1=ALU.mult).then_inc(s("w_fac"), 1)
            dve.wait_ge(s("w_fac"), 3)
            nc.vector.tensor_tensor(wsc[:, 7:8], wsc[:, 6:7], wsc[:, 3:4], ALU.mult).then_inc(s("w_fac"), 1)
            dve.wait_ge(s("l_init"), 4)
            with dve.Fori(0, H // ROWS) as i:
                for q in range(ROWS):
                    dve.wait_ge(s("l_res"), ROWS * i + q + 1)
                    for t in range(W):
                        slot = q * W + t
                        step = dve.snap(SLOTS * i + slot + 1)
                        dve.wait_ge(s("l_h"), step)
                        nc.vector.tensor_tensor(cand[:, :, 1], hr[:, (slot - 1) % SLOTS, :],
                                                cell[:, :, 1], ALU.mult).then_inc(s("l_hc"), 1)
                        dve.wait_ge(s("l_act"), step)
                        dve.wait_ge(s("l_hc"), step)
                        nc.vector.tensor_tensor_scan(cell[:, :, :].rearrange("p b k -> p (b k)"),
                                                     gate_i[:, :, :].rearrange("p b k -> p (b k)"),
                                                     cand[:, :, :].rearrange("p b k -> p (b k)"), 0.0,
                                                     ALU.mult, ALU.add).then_inc(s("l_c"), 1)
                        dve.wait_ge(s("l_oact"), step)
                        dve.wait_ge(s("l_tc"), step)
                        nc.vector.tensor_tensor(hr[:, slot, :], og[:, :], tcell[:, :], ALU.mult)\
                            .then_inc(s("l_h"), 1)

            norm(2)
            conv(1)

            dve.sem_inc(s("m_hid"), 2)
            dve.sem_inc(s("m_acc"), 4)
            norm(3)
            def col(k):
                return gt[:, k, :, :]

            def wide(a):
                return a.unsqueeze(2).broadcast_to([P, 16, E])

            red = [small[:, k, :] for k in range(8)]
            sm = [0]

            def note(ins):
                sm[0] += 1
                ins.then_inc(s("m_sm"), 1)
                dve.wait_ge(s("m_sm"), sm[0])

            rank = rank_c[:, :].unsqueeze(1).broadcast_to([P, 16, E])
            dve.wait_ge(s("m_log"), 1)
            logits = bank[6][:, 0:128].rearrange("p (g e) -> p g e", e=E)
            nc.vector.reduce_max(red[0], logits, AX.X).then_inc(s("m_max"), 1)
            dve.wait_ge(s("m_max"), 1)
            nc.vector.tensor_tensor(col(1), logits, wide(red[0]), ALU.subtract).then_inc(s("m_max"), 1)
            dve.wait_ge(s("m_exp"), 1)
            note(nc.vector.reduce_sum(red[1], col(0), AX.X))
            note(nc.vector.reciprocal(red[2], red[1]))
            note(nc.vector.tensor_tensor(col(2), col(0), wide(red[2]), ALU.mult))
            note(nc.vector.reduce_max(red[3], col(2), AX.X))
            note(nc.vector.tensor_tensor(col(3), col(2), wide(red[3]), ALU.is_equal))
            note(nc.vector.tensor_tensor(col(4), col(3), rank, ALU.mult))
            note(nc.vector.reduce_max(red[4], col(4), AX.X))
            note(nc.vector.tensor_tensor(col(5), col(4), wide(red[4]), ALU.is_equal))
            note(nc.vector.scalar_tensor_tensor(out=col(6), in0=col(5), scalar=-2.0, in1=col(2),
                                                op0=ALU.mult, op1=ALU.add))
            note(nc.vector.reduce_max(red[5], col(6), AX.X))
            note(nc.vector.tensor_tensor(col(3), col(6), wide(red[5]), ALU.is_equal))
            note(nc.vector.tensor_tensor(col(4), col(3), rank, ALU.mult))
            note(nc.vector.reduce_max(red[4], col(4), AX.X))
            note(nc.vector.tensor_tensor(col(7), col(4), wide(red[4]), ALU.is_equal))
            note(nc.vector.scalar_tensor_tensor(out=red[6], in0=red[3], scalar=1e-9, in1=red[5],
                                                op0=ALU.add, op1=ALU.add))
            note(nc.vector.reciprocal(red[7], red[6]))
            note(nc.vector.tensor_tensor(col(5), col(5), wide(red[3]), ALU.mult))
            note(nc.vector.tensor_tensor(col(7), col(7), wide(red[5]), ALU.mult))
            note(nc.vector.tensor_tensor(col(5), col(5), col(7), ALU.add))
            note(nc.vector.tensor_tensor(g1[:, :, :, :].rearrange("p j h e -> p (j h) e"), col(5),
                                         wide(red[7]), ALU.mult))
            note(nc.vector.tensor_scalar(g1[:, :, :, :], g1[:, :, :, :], wsc[:, 7:8], None, ALU.mult))
            dve.wait_ge(s("m_zero"), 1)
            U = 2 * NCH * PT
            with dve.Fori(0, PAIRS // 2) as i:
                def gather(g, n):
                    k = n // 2
                    dve.wait_ge(s("m_y"), 2 * NCH * i + g + 1)
                    dve.wait_ge(s("m_acc"), 4 * NCH * i + 2 * g + k + 4)
                    for jj in range(n % 2 * 2, n % 2 * 2 + 2):
                        j, hf = g % 2 * JJ + jj, g // 2 % 2
                        mm = nc.vector.scalar_tensor_tensor(
                            out=acc[:, j, hf, :],
                            in0=bank[4 + 2 * (g % 2) + jj // 2][:, (2 * (jj % 2) + k) * 128:][:, 0:128],
                            scalar=ge[:, g // NCH, j, hf, k:k + 1], in1=acc[:, j, hf, :],
                            op0=ALU.mult, op1=ALU.add)
                    if n % 2 == 1:
                        mm.then_inc(s("m_acc"), 1)

                dve.wait_ge(s("m_acc"), 4 * NCH * i + 4)
                for q in range(2):
                    nc.vector.tensor_copy(ge[:, q, :, :, :], g1[:, :, :, bass.ds(4 * i + 2 * q, 2)])\
                        .then_inc(s("m_ge"), 1)
                dve.wait_ge(s("m_ge"), 2 * i + 2)
                for u in range(U):
                    dve.wait_ge(s("m_silu"), U * i + u + 1)
                    dve.wait_ge(s("m_h"), 2 * U * i + 2 * u + 2)
                    nc.vector.scalar_tensor_tensor(out=hid[:, u % MR, :], in0=bank[2 + u % 2][:, :],
                                                   scalar=wsc[:, 5:6], in1=silu[:, u % 2, :],
                                                   op0=ALU.mult, op1=ALU.mult).then_inc(s("m_hid"), 1)
                    if MLAG <= u % PT < MLAG + 4 and u > PT:
                        gather(u // PT - 1, u % PT - MLAG)
                for n in range(4):
                    gather(2 * NCH - 1, n)
            dve.wait_ge(s("m_acc"), 4 + 2 * NCH * PAIRS)
            parts = acc.rearrange("p j h (k c) -> p (j h) k c", k=2)
            for q in range(2):
                half = slice(8 * q, 8 * q + 8)
                nc.vector.tensor_tensor(sq[:, q * 512:q * 512 + 512].rearrange("p (g c) -> p g c", c=C),
                                        parts[:, half, 0, :], parts[:, half, 1, :], ALU.add).then_inc(s("m_sum"), 1)
            for q in range(2):
                dve.wait_ge(s("m_tr"), q + 1)
                nc.vector.tensor_tensor(xs[:, q * 512:q * 512 + 512], xs[:, q * 512:q * 512 + 512],
                                        bank[6 + q][:, :], ALU.add).then_inc(s("m_out"), 1)


def kernel(**inputs):
    import numpy as np
    import concourse.bacc as bacc
    from concourse.bass_utils import run_bass_kernel_spmd

    a = {k: np.asarray(v) for k, v in inputs.items()}
    f = np.float32

    q = np.arange(P)
    pos = np.arange(16)
    tap = np.arange(TAPS)
    cy = 8 * np.arange(2)[None, :, None, None] + (q // W)[:, None, None, None] - 1 \
        + (tap // 3)[None, None, :, None] - pos
    cx = 0 * cy + (q % W)[:, None, None, None] - 1 + (tap % 3)[None, None, :, None] - pos
    tents = np.stack([cy, cx], 2).reshape(P, -1)
    mean = np.kron(np.eye(2), np.ones((C, C))) / C
    rank = np.tile(E - np.arange(E), (P, 1))
    consts = np.concatenate([mean, np.eye(P), rank, tents], 1).astype(f)

    def halves(t, fill):
        return np.stack([np.concatenate([t, fill], 0), np.concatenate([fill, t], 0)], 1)

    def conv_weights(w, order):
        w = w[order]
        main = np.stack([w[:, :, ky, kx] for ky in range(3) for kx in (0, 2)], 0)
        zero = np.zeros_like(w[:, :, 0, 0])
        side = np.stack([t for ky in range(3) for t in (w[:, :, ky, 1], zero)], 0)
        return halves(main.transpose(2, 0, 1), side.transpose(2, 0, 1))

    def sample_weights(w):
        t = w.transpose(1, 2, 3, 0).reshape(C, TAPS * C)
        return halves(t, np.zeros_like(t))

    split_yx = list(range(27))
    pairs_yx = list(range(0, 18, 2)) + list(range(1, 18, 2)) + list(range(18, 27))
    conv_w = np.stack([conv_weights(a["L0_conv_w_off"], split_yx), conv_weights(a["L1_conv_offset_w"], pairs_yx)])
    conv_b = np.stack([a["L0_conv_b_off"], a["L1_conv_offset_b"][pairs_yx]], 1)
    sample_w = np.stack([sample_weights(a["L0_conv_w"]), sample_weights(a["L1_conv_dcn_w"])])
    bn = np.stack([a["L0_conv_" + k] for k in ("gamma", "beta", "run_mean", "run_var", "b", "b")], 1)
    bn = np.concatenate([bn, bn], 0)
    gates = ("c", "i", "o")
    u = np.concatenate([a["L0_ffn_U_" + k] for k in gates], 1)
    lstm_u = halves(u, np.zeros_like(u))
    lstm_v = np.concatenate([a["L0_ffn_V_" + k] for k in gates], 1)
    lstm_b = np.concatenate([a["L0_ffn_b_" + k] for k in gates])[None]
    router = np.zeros((P, 2, E), f)
    router[:C, 0], router[C:, 1] = a["L1_ffn_router_w"].T, a["L1_ffn_router_w"].T
    full = FT * 128
    w13 = np.zeros((PAIRS, C, 2, PH), f)
    w2 = np.zeros((PAIRS, W2B, 128, C), f)
    for e in range(E):
        pr, k = e // 2, e % 2
        tail = 2 * full + k * REST
        for m, name in enumerate(("w1", "w3")):
            w = a["L1_ffn_" + name][e].T
            w13[pr, :, m, k * full:(k + 1) * full] = w[:, :full]
            w13[pr, :, m, tail:tail + REST] = w[:, full:]
        w = a["L1_ffn_w2"][e].T
        w2[pr, k * FT:(k + 1) * FT] = w[:full].reshape(FT, 128, C)
        w2[pr, 2 * FT + k, k * REST:(k + 1) * REST] = w[full:]
    w2 = w2.transpose(0, 2, 1, 3).reshape(PAIRS, 128, W2B * C)

    arrays = dict(x=a["x"], consts=consts, conv_w=conv_w, conv_b=conv_b, sample_w=sample_w, bn=bn,
                  lstm_u=lstm_u, lstm_v=lstm_v, lstm_b=lstm_b, router=router.reshape(P, 2 * E),
                  w13=w13.reshape(PAIRS, C, 2 * PH), w2=w2)
    arrays = {k: np.ascontiguousarray(v) for k, v in arrays.items()}
    nc = bacc.Bacc("TRN2", target_bir_lowering=False, num_devices=1)
    dram = {k: nc.dram_tensor(k, v.shape, F32, kind="ExternalInput").ap() for k, v in arrays.items()}
    out = nc.dram_tensor("out", (B, C, H, W), F32, kind="ExternalOutput").ap()
    split = lambda t: t.rearrange("(h b) c y x -> h c b (y x)", h=2)
    build(nc, split(dram["x"]), *[dram[k] for k in list(arrays)[1:]], split(out))
    r = run_bass_kernel_spmd(nc, [arrays], core_ids=[0])
    return r.results[0]["out"]
```

```python
from contextlib import ExitStack

import concourse.bass as bass
from concourse import mybir

F32 = mybir.dt.float32
F16 = mybir.dt.float16
I32 = mybir.dt.int32
ALU = mybir.AluOpType
ACT = mybir.ActivationFunctionType
AX = mybir.AxisListType

B, C, H, W = 8, 64, 16, 16
T = H * W
BQ = B // 2
COLS = BQ * T
P = 2 * C
TAPS = 9
OFF = 3 * TAPS
PW = W + 2
PADN = PW * PW
NP = 6
KG = 3
MATS = 2 * TAPS * 2
TG = 4
NG = MATS // TG
LAG = 4
NEXT = LAG - 1
TL = 5
RING = 3
SR = 6
SSCALE = 1024.0
ZTOP = 8
KTOP = 14
ROWS = 4
SLOTS = ROWS * W
E = 8
HID = 682
FT = HID // 128
REST = HID % 128
PAIRS = E // 2
PT = 2 * FT + 1
PH = PT * 128
W2B = PT + 1
MLAG = 3
MR = 4
XSCALE = 256.0
ZSCALE = 2.0 ** (ZTOP - KTOP) / XSCALE
WTOP = 14
HSCALE = 2.0 ** 15 / (2 * C) ** 2
NCH = 4
CH = B * T // NCH
JJ = CH // 128


def build(nc, x, consts, conv_w, conv_b, sample_w, bn, lstm_u, lstm_v, lstm_b, router, w13, w2, out):
    with ExitStack() as ctx:
        def sb(name, shape, dt=F32):
            return ctx.enter_context(nc.sbuf_tensor(name, shape, dt))

        def sem(name):
            return ctx.enter_context(nc.semaphore(name))

        bank = [ctx.enter_context(nc.psum_tensor(f"bank{i}", [P, 512], F32)) for i in range(8)]

        tent_c = sb("tent_c", [P, 2, 2, TAPS, 16])
        ident = sb("ident", [P, P])
        mean_w = sb("mean_w", [P, P])
        rank_c = sb("rank_c", [P, E])
        xs = sb("xs", [P, COLS])
        xn = sb("xn", [P, COLS + T])
        xc = sb("xc", [P, COLS])
        sq = sb("sq", [P, COLS])
        pad = [sb(f"pad{p}", [P, PADN]) for p in range(2)]
        convw = [sb(f"convw{l}", [P, 2, NP, OFF]) for l in range(2)]
        convb = sb("convb", [OFF, 2])
        samw = [sb(f"samw{l}", [P, TAPS * C]) for l in range(2)]
        samp = [sb(f"samp{l}", [P, 2, TAPS * C], F16) for l in range(2)]
        flat = [sb(f"flat{p}", [P, T], F16) for p in range(2)]
        bnp = sb("bnp", [P, 6])
        bnw = sb("bnw", [P, 6])
        om = sb("om", [OFF, T])
        omt = [sb(f"omt{p}", [P, 2, OFF]) for p in range(2)]
        sig = [sb(f"sig{p}", [P, 2, TAPS]) for p in range(2)]
        dist = sb("dist", [P, 2, 2 * TAPS, 16])
        ndist = sb("ndist", [P, 2, 2 * TAPS, 16])
        tent = [sb(f"tent{p}", [P, 2, 2 * TAPS, 16]) for p in range(2)]
        tentx = [sb(f"tentx{p}", [P, 2, TAPS, 16]) for p in range(2)]
        st = [sb(f"st{p}", [P, 2, TAPS, 256]) for p in range(2)]
        smat = sb("smat", [P, RING, TG, 128])
        shi = sb("shi", [P, SR, TG, 128], F16)
        zw = [sb(f"zw{p}", [P, 2, TAPS, 2, C], F16) for p in range(2)]
        osb = sb("osb", [P, 2, 2, 2, C])
        cmax = sb("cmax", [P, 2])
        cpow = sb("cpow", [1, 3, 2])
        csc = sb("csc", [P, 2, 2])
        ores = sb("ores", [P, T])
        lu = sb("lu", [P, 2, 192])
        lv = sb("lv", [C, 192])
        lb = sb("lb", [1, 192])
        ones = sb("ones", [1, 128])
        hr = sb("hr", [C, SLOTS, B])
        gate_i = sb("gate_i", [C, B, 2])
        cell = sb("cell", [C, B, 2])
        tcell = sb("tcell", [C, B])
        cand = sb("cand", [C, B, 2])
        og = sb("og", [C, B])
        hup = sb("hup", [P, 2, BQ, W])
        rw = sb("rw", [P, 2 * E])
        wmax = sb("wmax", [P, 2])
        wpow = sb("wpow", [1, 3, 2])
        wsc = sb("wsc", [P, 8])
        w13s = sb("w13s", [P, PAIRS, 2 * PH])
        wh = [sb(f"wh{q}", [P, 2 * PH], F16) for q in range(2)]
        wl = [sb(f"wl{q}", [P, 2 * PH], F16) for q in range(2)]
        w2f = sb("w2f", [P, PAIRS, W2B, C])
        w2p = [sb(f"w2p{q}", [P, W2B, 2, C], F16) for q in range(2)]
        hid = sb("hid", [P, MR, 512])

        def over(t, at, shape, dt=F32):
            n = 1
            for size in shape[1:]:
                n *= size
            flat = t.rearrange("p a b c -> p (a b c)")
            if dt == F16:
                return flat[:, at:at + n // 2].bitcast(F16)
            return flat[:, at:at + n]

        epsc = sb("epsc", [P, 2])
        dev = sb("dev", [P, 16])
        st0, st1 = st[0][:, :, :, :], st[1][:, :, :, :]
        xp = over(st0, 0, [P, 2 * COLS], F16)
        silu = over(st0, 1024, [P, 1024]).rearrange("p (u n) -> p u n", u=2)
        acc = over(st1, 0, [P, 2048]).rearrange("p (j h n) -> p j h n", j=8, h=2)
        slo = hid[:, 0:SR // 2, :].rearrange("p a b -> p (a b)").bitcast(F16) \
            .rearrange("p (s k n) -> p s k n", s=SR, k=TG)
        hh = zw[0][:, :, :, :, :].rearrange("p a b c d -> p (a b c d)")[:, 0:MR * 512] \
            .rearrange("p (u n) -> p u n", u=MR)
        hl = zw[1][:, :, :, :, :].rearrange("p a b c d -> p (a b c d)")[:, 0:MR * 512] \
            .rearrange("p (u n) -> p u n", u=MR)
        gt = xc[:, :].rearrange("p (k g e) -> p k g e", k=8, e=E)
        spare = smat[:, :, :, :].rearrange("p a b c -> p (a b c)")
        small = spare[:, 0:128].rearrange("p (k g) -> p k g", k=8)
        g1 = spare[:, 128:256].rearrange("p (j h e) -> p j h e", j=8, h=2)
        ge = spare[:, 256:320].rearrange("p (q j h k) -> p q j h k", q=2, j=8, h=2)

        def place(p, g):
            return (NG * p + g) % SR

        def waits(v):
            return not isinstance(v, int) or v > 0

        S = {}

        def s(name):
            if name not in S:
                S[name] = sem(name)
            return S[name]

        for l in range(2):
            for n in ("image", "taps", "conv_done", "om_sb", "omt_ps", "omt_sb", "z_ps", "z_act",
                      "z_dve", "sig", "tent", "st_ready", "tr_done", "tr_copied", "s_low", "sz_done",
                      "dist", "ndist", "tents", "osb", "out_ps", "out_sb", "res"):
                s(f"c{l}_{n}")
        for l in range(4):
            for n in ("mean", "xc", "sq", "var", "sd", "rs", "rb", "rt", "xn"):
                s(f"n{l}_{n}")
        for n in ("ld_const", "ld_mean", "ld_x", "ld_conv", "ld_lstm", "ld_w13", "ld_late", "ld_w2",
                  "zero", "bn_a", "bn_d", "tick", "tick_d", "tick_p",
                  "c_max", "c_tr", "c_pow", "c_bc", "c_scale",
                  "w_max", "w_tr", "w_pow", "w_bc", "w_scale", "w_fac", "w_high", "w_scaled", "w_stored",
                  "l_gi", "l_o", "l_act", "l_oact", "l_c", "l_tc", "l_h", "l_hc", "l_up", "l_res", "l_init",
                  "m_w0", "m_w1", "m_high", "m_scaled", "m_parts", "m_log", "m_max", "m_exp", "m_sm", "m_ge",
                  "m_h", "m_silu", "m_hid", "m_hh", "m_hl", "m_zero", "m_y", "m_acc", "m_sum", "m_tr",
                  "m_out", "st_out"):
            s(n)

        def pixels(t, p0, p1, b4):
            return t[p0:p1, bass.ts(b4, T)]

        block = ctx.enter_context(nc.Block())

        @block.sync
        def _(sp):
            for hf in range(2):
                sp.dma_start(xs[hf * C:hf * C + C, :].rearrange("c (b t) -> c b t", b=BQ), x[hf])\
                    .then_inc(s("ld_x"), 16)
            sp.dma_start(convw[0][:, :, :, :], conv_w[0]).then_inc(s("ld_conv"), 16)
            sp.dma_start(convb[:, :], conv_b).then_inc(s("ld_conv"), 16)
            sp.dma_start(samw[0][:, :], sample_w[0]).then_inc(s("ld_conv"), 16)
            sp.dma_start(bnp[:, :], bn).then_inc(s("ld_conv"), 16)
            sp.dma_start(rank_c[:, :], consts[:, 2 * P:2 * P + E]).then_inc(s("ld_const"), 16)
            sp.dma_start(tent_c[:, :, :, :, :].rearrange("p a b c d -> p (a b c d)"),
                         consts[:, 2 * P + E:]).then_inc(s("ld_const"), 16)
            sp.dma_start(convw[1][:, :, :, :], conv_w[1]).then_inc(s("ld_conv"), 16)
            sp.dma_start(samw[1][:, :], sample_w[1]).then_inc(s("ld_late"), 16)
            sp.dma_start(lu[:, :, :], lstm_u).then_inc(s("ld_lstm"), 16)
            sp.dma_start(lv[:, :], lstm_v).then_inc(s("ld_lstm"), 16)
            sp.dma_start(lb[:, :], lstm_b).then_inc(s("ld_lstm"), 16)
            sp.dma_start(rw[:, :], router).then_inc(s("ld_late"), 16)
            for e in range(PAIRS):
                for hf in range(2):
                    sp.dma_start(w13s[hf * C:hf * C + C, e, :], w13[e]).then_inc(s("ld_w13"), 16)
            for e in range(PAIRS):
                sp.dma_start(w2f[:, e, :, :], w2[e]).then_inc(s("ld_w2"), 16)
            def parts(q):
                kept = w13s[:, 2 + q, :].bitcast(F16).rearrange("p (k n) -> p k n", k=2)
                kept2 = w2f[:, 2 + q, :, :].rearrange("p a c -> p (a c)").bitcast(F16)
                used2 = w2p[q][:, :, :, :].rearrange("p a k c -> p (a k c)")
                return ((kept[:, 0, :], wh[q][:, :]), (kept[:, 1, :], wl[q][:, :]), (kept2, used2))

            for q in range(2):
                sp.wait_ge(s(f"m_w{q}"), 48)
                for kept, used in parts(q):
                    sp.dma_start(kept, used).then_inc(s("w_stored"), 16)
            for q in range(2):
                sp.wait_ge(s("w_stored"), 96)
                sp.wait_ge(s("m_h"), 2 * NCH * PT * (q + 1))
                sp.wait_ge(s("m_y"), NCH * (q + 1))
                for kept, used in parts(q):
                    sp.dma_start(used, kept).then_inc(s(f"m_w{q}"), 16)
            for q in range(2):
                sp.wait_ge(s("m_out"), q + 1)
                for hf in range(2):
                    sp.dma_start(out[hf][:, 2 * q:2 * q + 2, :],
                                 xs[hf * C:hf * C + C, q * 512:q * 512 + 512]
                                 .rearrange("c (b t) -> c b t", b=2)).then_inc(s("st_out"), 16)
            sp.wait_ge(s("st_out"), 64)

        @block.tensor
        def _(pe):
            def norm(l, ready, middle=None, end=None):
                for wait_sem, v in ready:
                    pe.wait_ge(s(wait_sem), v)
                for j in range(2):
                    nc.tensor.matmul(bank[j][:, :], mean_w[:, :], xs[:, j * 512:j * 512 + 512],
                                     start=True, stop=True).then_inc(s(f"n{l}_mean"), 1)
                for j in range(8):
                    if j % 4 == 0:
                        pe.wait_ge(s(f"n{l}_sq"), j // 4 + 1)
                    mm = nc.tensor.matmul(bank[2][:, 2 * j:2 * j + 2], sq[:, j * 128:j * 128 + 128],
                                          mean_w[:, 0:P:C], start=(j == 0), stop=True, skip_group_check=True)
                mm.then_inc(s(f"n{l}_var"), 1)
                if middle:
                    middle()
                pe.wait_ge(s(f"n{l}_rb"), 1)
                for j in range(8):
                    mm = nc.tensor.transpose(bank[j // 4][:, j % 4 * 128:j % 4 * 128 + 128],
                                             sq[:, j * 128:j * 128 + 128], ident[:, :])
                    if j % 4 == 3:
                        mm.then_inc(s(f"n{l}_rt"), 1)
                if end:
                    end()

            def conv(l):
                c = f"c{l}_"
                pe.sem_inc(s(c + "tr_done"), 1 + NG)
                pe.sem_inc(s(c + "sz_done"), 1)
                pe.sem_inc(s(c + "out_ps"), 1)

                def offsets(m, p, half):
                    if half == 0:
                        pe.wait_ge(s(c + "image"), 4 * m + 4)
                        pe.wait_ge(s(c + "omt_sb"), m)
                    img = pad[p][:, :].rearrange("p (y x) -> p y x", x=PW)
                    for j in range(half * NP // 2, (half + 1) * NP // 2):
                        ky, kx = j // 2, 2 * (j % 2)
                        mm = nc.tensor.matmul(bank[0][0:OFF, 0:T], convw[l][:, p, j, :],
                                              img[:, ky:ky + H, kx:kx + W], start=(j == 0), stop=(j == NP - 1))
                    if half == 1:
                        mm.then_inc(s(c + "conv_done"), 1)

                def turn_offsets(m):
                    pe.wait_ge(s(c + "om_sb"), m + 1)
                    pe.sem_inc(s("tick_p"), 1)
                    for t in range(2):
                        mm = nc.tensor.transpose(bank[0][:, 256 + t * OFF:256 + (t + 1) * OFF],
                                                 om[:, t * 128:t * 128 + 128], ident[0:OFF, 0:OFF])
                    mm.then_inc(s(c + "omt_ps"), 1)

                def taps(m, p, half):
                    pe.wait_ge(s(c + "z_dve"), 4 * m + 2 * half)
                    src = flat[p][:, half * 128:half * 128 + 128]
                    for j, k0, k1 in ((0, 0, TL), (1, TL, TAPS)):
                        for part in range(2):
                            mm = nc.tensor.matmul(bank[1 + j][:, 0:(k1 - k0) * C], src,
                                                  samp[l][:, part, k0 * C:k1 * C],
                                                  start=(part == 0), stop=(part == 1))
                        mm.then_inc(s(c + "z_ps"), 1)

                def turn_weights(m, p, g):
                    last = TG * g + TG - 1
                    pe.wait_ge(s(c + "st_ready"), 1 + 6 * m + last // (2 * KG) + 1)
                    if waits(NG * m + g - RING + 2):
                        pe.wait_ge(s(c + "tr_copied"), NG * m + g - RING + 2)
                    for k in range(TG):
                        t, tap, half = (TG * g + k) // 18, (TG * g + k) % 18 // 2, k % 2
                        mm = nc.tensor.transpose(bank[3 + g % RING][:, k * 128:k * 128 + 128],
                                                 st[p][:, t, tap, half * 128:half * 128 + 128], ident[:, :])
                    mm.then_inc(s(c + "tr_done"), 1)

                def sums(m, p, h):
                    pe.wait_ge(s(c + "s_low"), NG * m + h + 1)
                    if h == 0:
                        pe.wait_ge(s(c + "z_dve"), 4 * m + 4)
                    for k in range(TG):
                        a = TG * h + k
                        t, tap, half = a // 18, a % 18 // 2, k % 2
                        lo = (2 * p + t) * 2 * C
                        for part in (shi, slo):
                            mm = nc.tensor.matmul(bank[6][:, lo:lo + 2 * C], part[:, place(p, h), k, :],
                                                  zw[p][:, half, tap, :, :].rearrange("p k c -> p (k c)"),
                                                  start=(p == 0 and a == 0 and part is shi), stop=(a % 18 == 17),
                                                  skip_group_check=True)
                    mm.then_inc(s(c + "sz_done"), 1)

                def turn(i):
                    pe.wait_ge(s(c + "osb"), i + 1)
                    pe.wait_ge(s(c + "out_sb"), 1 + i)
                    for t in range(2):
                        for k in range(2):
                            mm = nc.tensor.matmul(bank[7][:, t * 128:t * 128 + 128],
                                                  osb[:, t, k, :, :].rearrange("p h c -> p (h c)"), ident[:, :],
                                                  start=(t == 0 and k == 0), stop=(k == 1), skip_group_check=True)
                    mm.then_inc(s(c + "out_ps"), 1)

                def stream(m, p, ended=None, first=False, last=False):
                    for g in range(NG):
                        if NEXT - 1 <= g <= NEXT and not last:
                            offsets(m + 1, 1 - p, g - NEXT + 1)
                        if g == NEXT + 1 and not last:
                            taps(m + 1, 1 - p, 0)
                            turn_offsets(m + 1)
                        if g == NEXT + 3 and not last:
                            taps(m + 1, 1 - p, 1)
                        if g == LAG + 2 and ended is not None:
                            turn(ended)
                        turn_weights(m, p, g)
                        if g >= LAG:
                            if g == LAG and ended is not None:
                                pe.wait_ge(s(c + "osb"), ended + 1)
                            sums(m, p, g - LAG)
                        elif not first:
                            sums(m - 1, 1 - p, NG - LAG + g)

                offsets(0, 0, 0)
                offsets(0, 0, 1)
                pe.wait_ge(s(c + "taps"), 2)
                taps(0, 0, 0)
                turn_offsets(0)
                taps(0, 0, 1)
                stream(0, 0, first=True)
                with pe.Fori(0, BQ - 1) as i:
                    stream(2 * i + 1, 1)
                    stream(2 * i + 2, 0, ended=i)
                stream(B - 1, 1, last=True)
                for h in range(NG - LAG, NG):
                    sums(B - 1, 1, h)
                turn(BQ - 1)

            pe.wait_ge(s("ld_mean"), 32)

            def turn_max():
                pe.wait_ge(s("c_max"), 2)
                for k in range(2):
                    nc.tensor.transpose(bank[3][0:1, k * 128:k * 128 + 128], cmax[:, k:k + 1], ident[:, :])\
                        .then_inc(s("c_tr"), 1)

            def spread():
                pe.wait_ge(s("l_init"), 1)
                pe.wait_ge(s("c_pow"), 3)
                nc.tensor.matmul(bank[3][:, 256:258], ones[:, :], cpow[:, 2, :], start=True, stop=True)\
                    .then_inc(s("c_bc"), 1)

            norm(0, [("ld_x", 32)], turn_max, spread)
            pe.wait_ge(s("ld_conv"), 16 * 5)
            pe.wait_ge(s("n0_xn"), 2)
            conv(0)

            norm(1, [("c0_res", 1 + BQ)])
            pe.wait_ge(s("ld_lstm"), 16 * 3)
            pe.wait_ge(s("n1_xn"), 2)
            pe.wait_ge(s("w_max"), 2)
            for k in range(2):
                nc.tensor.transpose(bank[4][0:1, k * 128:k * 128 + 128], wmax[:, k:k + 1], ident[:, :])\
                    .then_inc(s("w_tr"), 1)
            pe.wait_ge(s("l_init"), 4)

            def gates_x(r, q, k):
                bk, lo, m = ((bank[q], 0, 128), (bank[2 + q], 128, C))[k // 3]
                if k % 3 == 0:
                    nc.tensor.matmul(bk[0:m, 0:128], lb[:, lo:lo + m], ones[:, :],
                                     start=True, stop=False, skip_group_check=True)
                else:
                    hf = k % 3 - 1
                    rhs = xn[:, bass.ds(r * W, COLS)].rearrange("p (b t) -> p b t", b=BQ)[:, :, 0:W]
                    nc.tensor.matmul(bk[0:m, hf * C:hf * C + C], lu[:, hf, lo:lo + m], rhs,
                                     start=False, stop=False, skip_group_check=True)

            for k in range(6):
                gates_x(0, 0, k)
            pe.wait_ge(s("w_pow"), 3)
            nc.tensor.matmul(bank[5][:, 0:2], ones[:, :], wpow[:, 2, :], start=True, stop=True)\
                .then_inc(s("w_bc"), 1)
            with pe.Fori(0, H // ROWS) as i:
                for q in range(ROWS):
                    for t in range(W):
                        slot = q * W + t
                        step = pe.snap(SLOTS * i + slot + 1)
                        pe.wait_ge(s("l_h"), step)
                        prev = hr[:, (slot - 1) % SLOTS, :]
                        gi = bank[q % 2][:, 0:128].rearrange("p (b t) -> p t b", t=W)[:, t, :]
                        go = bank[2 + q % 2][0:C, 0:128].rearrange("p (b t) -> p t b", t=W)[:, t, :]
                        nc.tensor.matmul(gi, lv[:, 0:128], prev, start=False, stop=True,
                                         skip_group_check=True).then_inc(s("l_gi"), 1)
                        nc.tensor.matmul(go, lv[:, 128:192], prev, start=False, stop=True,
                                         skip_group_check=True).then_inc(s("l_o"), 1)
                        if 4 <= t < 10:
                            gates_x(ROWS * i + q + 1, 1 - q % 2, t - 4)

            pe.wait_ge(s("ld_late"), 32)
            norm(2, [("l_res", H + ROWS)])
            pe.wait_ge(s("n2_xn"), 2)
            conv(1)

            norm(3, [("c1_res", 1 + BQ)])
            for j in range(8):
                if j % 4 == 0:
                    pe.wait_ge(s("n3_xn"), j // 4 + 1)
                mm = nc.tensor.matmul(bank[6][:, j * 16:j * 16 + 16], xn[:, j * 128:j * 128 + 128], rw[:, :],
                                      start=(j == 0), stop=True, skip_group_check=True)
            mm.then_inc(s("m_log"), 1)
            pe.wait_ge(s("m_parts"), 2)
            U = 2 * NCH * PT
            with pe.Fori(0, PAIRS // 2) as i:
                def first(u):
                    q, ch, k0 = u // (NCH * PT), u // PT % NCH, u % PT * 128
                    tok = slice(ch * CH, ch * CH + CH)
                    if u % (NCH * PT) == 0:
                        pe.wait_ge(s(f"m_w{q}"), 48 * i + 96)
                    pe.wait_ge(s("m_hid"), U * i + u + 1)
                    for k in range(2):
                        col = k * PH + k0
                        bk = bank[2 * k + u % 2]
                        nc.tensor.matmul(bk[:, :], wh[q][:, col:col + 128], xp[:, tok], start=True, stop=False)
                        nc.tensor.matmul(bk[:, :], wl[q][:, col:col + 128], xp[:, tok], start=False, stop=True)\
                            .then_inc(s("m_h"), 1)

                def second(u):
                    q, g, t = u // (NCH * PT), u // PT, u % PT
                    if t == 0:
                        pe.wait_ge(s("m_acc"), 4 * NCH * i + 2 * g + 2)
                    pe.wait_ge(s("m_hl"), U * i + u + 1)
                    k, n = (t // FT, 2 * C) if t < 2 * FT else (0, 4 * C)
                    rhs = w2p[q][:, t:t + n // (2 * C), :, :].rearrange("p a k c -> p (a k c)")
                    for j in range(JJ):
                        lo = j % 2 * 4 * C + k * 2 * C
                        for part in (hh, hl):
                            mm = nc.tensor.matmul(bank[4 + 2 * (g % 2) + j // 2][:, lo:lo + n],
                                                  part[:, u % MR, j * 128:j * 128 + 128], rhs,
                                                  start=(t == 0 and j % 2 == 0 and part is hh),
                                                  stop=(t == PT - 1), skip_group_check=True)
                    if t == PT - 1:
                        mm.then_inc(s("m_y"), 1)

                for u in range(U + MLAG):
                    if u < U:
                        first(u)
                    if u >= MLAG:
                        second(u - MLAG)
            for j in range(8):
                if j % 4 == 0:
                    pe.wait_ge(s("m_sum"), j // 4 + 1)
                mm = nc.tensor.transpose(bank[6 + j // 4][:, j % 4 * 128:j % 4 * 128 + 128],
                                         sq[:, j * 128:j * 128 + 128], ident[:, :])
                if j % 4 == 3:
                    mm.then_inc(s("m_tr"), 1)

        @block.scalar
        def _(act):
            act.dma_start(mean_w[:, :], consts[:, 0:P]).then_inc(s("ld_mean"), 16)
            act.dma_start(ident[:, :], consts[:, P:2 * P]).then_inc(s("ld_mean"), 16)
            def norm(l, eps):
                for j in range(2):
                    col = slice(j * 512, j * 512 + 512)
                    act.wait_ge(s(f"n{l}_xc"), j + 1)
                    nc.scalar.activation(sq[:, col], xc[:, col], ACT.Square).then_inc(s(f"n{l}_sq"), 1)
                act.wait_ge(s(f"n{l}_var"), 1)
                nc.scalar.activation(dev[:, :], bank[2][:, 0:16], ACT.Sqrt, bias=epsc[:, eps:eps + 1])\
                    .then_inc(s(f"n{l}_sd"), 1)

            def conv(l):
                c = f"c{l}_"

                act.sem_inc(s(c + "tr_copied"), 1)
                act.sem_inc(s(c + "out_sb"), 1)

                def offsets(m):
                    act.wait_ge(s(c + "conv_done"), m + 1)
                    nc.scalar.activation(om[:, :], bank[0][0:OFF, 0:T], ACT.Identity,
                                         bias=convb[:, l:l + 1]).then_inc(s(c + "om_sb"), 1)

                def taps(m, p, half):
                    for j, k0, k1 in ((0, 0, TL), (1, TL, TAPS)):
                        act.wait_ge(s(c + "z_ps"), 4 * m + 2 * half + j + 1)
                        nc.scalar.activation(zw[p][:, half, k0:k1, 0, :],
                                             bank[1 + j][:, 0:(k1 - k0) * C].rearrange("p (k c) -> p k c", c=C),
                                             ACT.Copy, scale=ZSCALE).then_inc(s(c + "z_act"), 1)

                def turned(m, p):
                    if not (isinstance(m, int) and m == 0):
                        act.wait_ge(s(c + "tent"), 1 + m - 1)
                    act.wait_ge(s(c + "omt_ps"), m + 1)
                    nc.scalar.copy(omt[p][:, :, :].rearrange("p t k -> p (t k)"), bank[0][:, 256:256 + 2 * OFF])\
                        .then_inc(s(c + "omt_sb"), 1)
                    act.wait_ge(s(c + "omt_sb"), m + 1)
                    nc.scalar.activation(sig[p][:, :, :], omt[p][:, :, 2 * TAPS:OFF], ACT.Sigmoid)\
                        .then_inc(s(c + "sig"), 1)

                def copy(m, p, g):
                    act.wait_ge(s(c + "tr_done"), 1 + NG * (m + 1) + g + 1)
                    if waits(NG * m + g - SR + 2):
                        act.wait_ge(s(c + "sz_done"), NG * m + g - SR + 2)
                    nc.scalar.activation(shi[:, place(p, g), :, :].rearrange("p k n -> p (k n)"),
                                         bank[3 + g % RING][:, :], ACT.Copy, scale=SSCALE)
                    if waits(NG * m + g - RING + 1):
                        act.wait_ge(s(c + "s_low"), NG * m + g - RING + 1)
                    nc.scalar.activation(smat[:, g % RING, :, :].rearrange("p k n -> p (k n)"),
                                         bank[3 + g % RING][:, :], ACT.Copy, scale=SSCALE)\
                        .then_inc(s(c + "tr_copied"), 1)

                def summed(i):
                    act.wait_ge(s(c + "sz_done"), 1 + NG * (2 * i + 2))
                    act.wait_ge(s(c + "out_ps"), 1 + i)
                    for p in range(2):
                        ins = nc.scalar.copy(osb[:, :, :, p, :],
                                             bank[6][:, p * 256:p * 256 + 256]
                                             .rearrange("p (t k c) -> p t k c", t=2, k=2))
                    ins.then_inc(s(c + "osb"), 1)

                def result(i):
                    act.wait_ge(s(c + "out_ps"), 1 + i + 1)
                    act.wait_ge(s(c + "res"), 1 + i)
                    if l == 0:
                        nc.scalar.activation(ores[:, :], bank[7][:, 0:T], ACT.Relu, scale=bnw[:, 0:1],
                                             bias=bnw[:, 4:5]).then_inc(s(c + "out_sb"), 1)
                    else:
                        nc.scalar.activation(ores[:, :], bank[7][:, 0:T], ACT.Copy, scale=csc[:, 1, 1:2])\
                            .then_inc(s(c + "out_sb"), 1)

                def stream(m, p, ended=None, last=False):
                    for g in range(NG):
                        if g == NEXT and not last:
                            offsets(m + 1)
                        if g == NEXT + 1 and ended is not None:
                            summed(ended)
                        if g == NEXT + 1 and not last:
                            taps(m + 1, 1 - p, 0)
                            turned(m + 1, 1 - p)
                        if g == NEXT + 3 and not last:
                            taps(m + 1, 1 - p, 1)
                        if g == LAG + 3 and ended is not None:
                            result(ended)
                        copy(m, p, g)

                offsets(0)
                taps(0, 0, 0)
                turned(0, 0)
                taps(0, 0, 1)
                stream(0, 0)
                with act.Fori(0, BQ - 1) as i:
                    stream(2 * i + 1, 1)
                    stream(2 * i + 2, 0, ended=i)
                stream(B - 1, 1, last=True)
                summed(BQ - 1)
                result(BQ - 1)

            act.wait_ge(s("zero"), 4)
            norm(0, 0)
            act.wait_ge(s("ld_conv"), 16 * 5)
            nc.scalar.activation(bnw[:, 0:1], bnp[:, 3:4], ACT.Sqrt, bias=epsc[:, 1:2]).then_inc(s("bn_a"), 1)
            act.wait_ge(s("bn_d"), 6)
            act.wait_ge(s("c_scale"), 2)
            conv(0)

            norm(1, 1)
            act.wait_ge(s("l_init"), 4)
            with act.Fori(0, H // ROWS) as i:
                for q in range(ROWS):
                    for t in range(W):
                        slot = q * W + t
                        gates = bank[q % 2][:, 0:128].rearrange("p (b t) -> p t b", t=W)[:, t, :]
                        gate_o = bank[2 + q % 2][0:C, 0:128].rearrange("p (b t) -> p t b", t=W)[:, t, :]
                        step = act.snap(SLOTS * i + slot + 1)
                        act.wait_ge(s("l_gi"), step)
                        nc.scalar.activation(gate_i[:, :, 1], gates[C:P, :], ACT.Sigmoid)
                        nc.scalar.activation(cand[:, :, 0], gates[0:C, :], ACT.Tanh).then_inc(s("l_act"), 1)
                        act.wait_ge(s("l_o"), step)
                        nc.scalar.activation(og[:, :], gate_o, ACT.Sigmoid).then_inc(s("l_oact"), 1)
                        act.wait_ge(s("l_c"), step)
                        nc.scalar.activation(tcell[:, :], cell[:, :, 1], ACT.Tanh).then_inc(s("l_tc"), 1)

            norm(2, 0)
            conv(1)

            norm(3, 1)
            act.wait_ge(s("n3_xn"), 2)
            for hf in range(2):
                nc.scalar.activation(xp[hf * C:hf * C + C, hf * COLS:hf * COLS + COLS],
                                     xn[hf * C:hf * C + C, 0:COLS], ACT.Copy, scale=XSCALE)\
                    .then_inc(s("m_high"), 1)
            nc.scalar.activation(sq[:, :], xn[:, 0:COLS], ACT.Copy, scale=XSCALE).then_inc(s("m_scaled"), 1)
            act.wait_ge(s("m_max"), 2)
            nc.scalar.activation(gt[:, 0, :, :], gt[:, 1, :, :], ACT.Exp).then_inc(s("m_exp"), 1)
            U = 2 * NCH * PT
            with act.Fori(0, PAIRS // 2) as i:
                def high(u):
                    act.wait_ge(s("m_hid"), U * i + u + 3)
                    nc.scalar.copy(hh[:, u % MR, :], hid[:, u % MR, :]).then_inc(s("m_hh"), 1)

                for u in range(U):
                    act.wait_ge(s("m_h"), 2 * U * i + 2 * u + 1)
                    nc.scalar.activation(silu[:, u % 2, :], bank[u % 2][:, :], ACT.Silu, scale=wsc[:, 4:5])\
                        .then_inc(s("m_silu"), 1)
                    if u > 0:
                        high(u - 1)
                high(U - 1)

        @block.gpsimd
        def _(gp):
            for p in range(2):
                nc.gpsimd.memset(pad[p][:, :], 0.0).then_inc(s("zero"), 1)
            nc.gpsimd.memset(epsc[:, 0:1], 1e-6).then_inc(s("zero"), 1)
            nc.gpsimd.memset(epsc[:, 1:2], 1e-5).then_inc(s("zero"), 1)

            def conv(l):
                c = f"c{l}_"

                def add(i):
                    gp.wait_ge(s(c + "out_sb"), 1 + i + 1)
                    gp.sem_inc(s("tick"), 1)
                    nc.gpsimd.tensor_tensor(pixels(xs, 0, P, i), pixels(xs, 0, P, i), ores[:, :], ALU.add)\
                        .then_inc(s(c + "res"), 1)

                def low(m, p):
                    for g in range(NG):
                        gp.wait_ge(s(c + "tr_copied"), 1 + NG * m + g + 1)
                        nc.gpsimd.tensor_tensor(slo[:, place(p, g), :, :], smat[:, g % RING, :, :],
                                                shi[:, place(p, g), :, :], ALU.subtract).then_inc(s(c + "s_low"), 1)

                gp.sem_inc(s(c + "res"), 1)
                low(0, 0)
                with gp.Fori(0, BQ - 1) as i:
                    low(2 * i + 1, 1)
                    low(2 * i + 2, 0)
                    add(i)
                low(B - 1, 1)
                add(BQ - 1)

            def split(q, n, full, high, low, scale):
                nc.gpsimd.tensor_tensor(high, full, scale, ALU.mult).then_inc(s("w_high"), 1)
                gp.wait_ge(s("w_high"), n)
                nc.gpsimd.tensor_tensor(full, full, scale, ALU.mult).then_inc(s("w_scaled"), 1)
                gp.wait_ge(s("w_scaled"), n)
                nc.gpsimd.tensor_tensor(low, full, high, ALU.subtract).then_inc(s(f"m_w{q}"), 24)

            def split_pair(e, q, n):
                split(q, n, w13s[:, e, :], wh[q][:, :], wl[q][:, :], wsc[:, 0:1].broadcast_to([P, 2 * PH]))
                split(q, n + 1, w2f[:, e, :, :], w2p[q][:, :, 0, :], w2p[q][:, :, 1, :],
                      wsc[:, 1:2].unsqueeze(2).broadcast_to([P, W2B, C]))

            conv(0)
            gp.sem_inc(s("l_res"), ROWS)
            gp.wait_ge(s("w_scale"), 2)
            gp.wait_ge(s("ld_w2"), 16 * PAIRS)
            for q in range(2):
                split_pair(2 + q, q, 2 * q + 1)
            gp.wait_ge(s("w_stored"), 96)
            for q in range(2):
                split_pair(q, q, 2 * q + 5)
            gp.wait_ge(s("m_w1"), 96)
            xsv = xs[:, :].rearrange("p (b t) -> p b t", b=BQ)
            with gp.Fori(0, H // ROWS) as i:
                for q in range(ROWS):
                    row = bass.ds((ROWS * i + q) * W, W)
                    gp.wait_ge(s("l_res"), ROWS * i + q + ROWS)
                    gp.wait_ge(s("l_h"), SLOTS * i + (q + 1) * W + 1)
                    gp.sem_inc(s("tick"), 1)
                    for hf in range(2):
                        nc.gpsimd.tensor_copy(hup[C * hf:C * hf + C, q % 2, :, :],
                                              hr[:, q * W:q * W + W, BQ * hf:BQ * hf + BQ].rearrange("p t b -> p b t"))\
                            .then_inc(s("l_up"), 1)
                    gp.wait_ge(s("l_up"), 2 * (ROWS * i + q + 1))
                    gp.sem_inc(s("tick"), 1)
                    nc.gpsimd.tensor_tensor(xsv[:, :, row], xsv[:, :, row], hup[:, q % 2, :, :], ALU.add)\
                        .then_inc(s("l_res"), 1)
            conv(1)
            gp.wait_ge(s("c1_out_ps"), 1 + BQ)
            nc.gpsimd.memset(acc, 0.0).then_inc(s("m_zero"), 1)
            gp.wait_ge(s("m_zero"), 1)
            for hf in range(2):
                src, dst = slice(hf * C, hf * C + C), slice(C - hf * C, 2 * C - hf * C)
                tok = slice(hf * COLS, hf * COLS + COLS)
                gp.wait_ge(s("m_high"), hf + 1)
                gp.wait_ge(s("m_scaled"), 1)
                if hf:
                    gp.wait_ge(s("m_parts"), hf)
                nc.gpsimd.tensor_tensor(xp[dst, tok], sq[src, :], xp[src, tok], ALU.subtract)\
                    .then_inc(s("m_parts"), 1)
            gp.wait_ge(s("m_parts"), 2)
            U = 2 * NCH * PT
            with gp.Fori(0, PAIRS // 2) as i:
                for u in range(U):
                    gp.wait_ge(s("m_hh"), U * i + u + 1)
                    nc.gpsimd.tensor_tensor(hl[:, u % MR, :], hid[:, u % MR, :], hh[:, u % MR, :], ALU.subtract)\
                        .then_inc(s("m_hl"), 1)

        @block.vector
        def _(dve):
            def norm(l, first=None, second=None):
                for j in range(2):
                    col = slice(j * 512, j * 512 + 512)
                    dve.wait_ge(s(f"n{l}_mean"), j + 1)
                    nc.vector.tensor_tensor(xc[:, col], xs[:, col], bank[j][:, :], ALU.subtract)\
                        .then_inc(s(f"n{l}_xc"), 1)
                if first:
                    first()
                dve.wait_ge(s(f"n{l}_sd"), 1)
                nc.vector.reciprocal(dev[:, :], dev[:, :]).then_inc(s(f"n{l}_rs"), 1)
                dve.wait_ge(s(f"n{l}_rs"), 1)
                nc.vector.tensor_copy(sq[:, :].rearrange("p (k c) -> p k c", c=C),
                                      dev[:, :].unsqueeze(2).broadcast_to([P, 16, C])).then_inc(s(f"n{l}_rb"), 1)
                if second:
                    second()
                for j in range(2):
                    col = slice(j * 512, j * 512 + 512)
                    dve.wait_ge(s(f"n{l}_rt"), j + 1)
                    nc.vector.tensor_tensor(xn[:, col], xc[:, col], bank[j][:, :], ALU.mult)\
                        .then_inc(s(f"n{l}_xn"), 1)

            def conv(l):
                c = f"c{l}_"

                def tap_images(m, p, half):
                    for j, k0, k1 in ((0, 0, TL), (1, TL, TAPS)):
                        dve.wait_ge(s(c + "z_act"), 4 * m + 2 * half + j + 1)
                        nc.vector.scalar_tensor_tensor(
                            out=zw[p][:, half, k0:k1, 1, :],
                            in0=bank[1 + j][:, 0:(k1 - k0) * C].rearrange("p (k c) -> p k c", c=C),
                            scalar=ZSCALE, in1=zw[p][:, half, k0:k1, 0, :],
                            op0=ALU.mult, op1=ALU.subtract).then_inc(s(c + "z_dve"), 1)

                def offsets(m, p):
                    tap_images(m, p, 0)
                    dve.wait_ge(s(c + "omt_sb"), m + 1)
                    shift = omt[p][:, :, 0:2 * TAPS].unsqueeze(3).broadcast_to([P, 2, 2 * TAPS, 16])
                    nc.vector.tensor_tensor(dist[:, :, :, :], tent_c[:, :, :, :, :].rearrange("p t a k n -> p t (a k) n"),
                                            shift, ALU.add).then_inc(s(c + "dist"), 1)
                    dve.wait_ge(s(c + "dist"), m + 1)
                    nc.vector.scalar_tensor_tensor(out=ndist[:, :, :, :], in0=dist[:, :, :, :], scalar=-1.0,
                                                   in1=dist[:, :, :, :], op0=ALU.mult, op1=ALU.min)\
                        .then_inc(s(c + "ndist"), 1)
                    dve.wait_ge(s(c + "ndist"), m + 1)
                    dve.wait_ge(s(c + "st_ready"), 1 + 6 * m)
                    nc.vector.tensor_scalar(tent[p][:, :, :, :], ndist[:, :, :, :], 1.0, 0.0, ALU.add, ALU.max)\
                        .then_inc(s(c + "tents"), 1)
                    tap_images(m, p, 1)
                    dve.wait_ge(s(c + "tents"), m + 1)
                    dve.wait_ge(s(c + "sig"), m + 1)
                    nc.vector.tensor_tensor(tentx[p][:, :, :, :], tent[p][:, :, TAPS:2 * TAPS, :],
                                            sig[p][:, :, :].unsqueeze(3).broadcast_to([P, 2, TAPS, 16]), ALU.mult)\
                        .then_inc(s(c + "tent"), 1)

                def image(m, p, b4):
                    if not (isinstance(m, int) and m < 2):
                        dve.wait_ge(s(c + "z_ps"), 4 * (m - 1))
                        dve.sem_inc(s("tick_d"), 1)
                    own, other = C * p, C * (1 - p)
                    src = pixels(xn, own, own + C, b4).rearrange("c (y x) -> c y x", x=W)
                    for lo, x0 in ((own, 1), (other, 0)):
                        dst = pad[p][lo:lo + C, :].rearrange("c (y x) -> c y x", x=PW)
                        nc.vector.tensor_copy(dst[:, 1:1 + H, x0:x0 + W], src).then_inc(s(c + "image"), 1)
                    whole = pixels(xn, own, own + C, b4)
                    nc.vector.tensor_scalar(flat[p][own:own + C, :], whole, XSCALE, None, ALU.mult)\
                        .then_inc(s(c + "image"), 1)
                    dve.wait_ge(s(c + "image"), 4 * m + 3)
                    nc.vector.scalar_tensor_tensor(out=flat[p][other:other + C, :], in0=whole, scalar=XSCALE,
                                                   in1=flat[p][own:own + C, :], op0=ALU.mult, op1=ALU.subtract)\
                        .then_inc(s(c + "image"), 1)

                def outer(m, p):
                    dve.wait_ge(s(c + "tent"), 1 + m + 1)
                    dve.wait_ge(s(c + "tr_done"), 1 + NG * m)
                    for t in range(2):
                        for k in range(0, TAPS, KG):
                            ty = tent[p][:, t, k:k + KG, :].unsqueeze(3).broadcast_to([P, KG, 16, 16])
                            tx = tentx[p][:, t, k:k + KG, :].unsqueeze(2).broadcast_to([P, KG, 16, 16])
                            nc.vector.tensor_tensor(
                                st[p][:, t, k:k + KG, :].rearrange("p k (y x) -> p k y x", x=16), ty, tx, ALU.mult)\
                                .then_inc(s(c + "st_ready"), 1)

                dve.sem_inc(s(c + "tent"), 1)
                dve.sem_inc(s(c + "st_ready"), 1)
                dve.wait_ge(s(f"n{2 * l}_xn"), 2)
                dve.wait_ge(s("zero"), 2)
                image(0, 0, 0)
                split_taps(l)
                image(1, 1, 0)
                def batch(m, p, b4_next):
                    offsets(m, p)
                    outer(m, p)
                    if b4_next is not None:
                        image(m + 2, p, b4_next)

                with dve.Fori(0, BQ - 1) as i:
                    for p in range(2):
                        batch(2 * i + p, p, i + 1)
                for p in range(2):
                    batch(B - 2 + p, p, None)

            def largest():
                dve.wait_ge(s("ld_conv"), 80)
                dve.wait_ge(s("ld_late"), 32)
                for l in range(2):
                    nc.vector.tensor_reduce(cmax[:, l:l + 1], samw[l][:, :], AX.X,
                                            ALU.max, apply_absolute_value=True).then_inc(s("c_max"), 1)

            def power(name, pw, src, top):
                dve.wait_ge(s(f"{name}_tr"), 2)
                nc.vector.reduce_max(pw[:, 0, :], src[0:1, 0:256].rearrange("p (k n) -> p k n", k=2), AX.X)\
                    .then_inc(s(f"{name}_pow"), 1)
                dve.wait_ge(s(f"{name}_pow"), 1)
                nc.vector.tensor_scalar(pw[:, 1, :], pw[:, 0, :], 2.0 ** -100, 2.0 ** -top, ALU.max, ALU.mult)\
                    .then_inc(s(f"{name}_pow"), 1)
                dve.wait_ge(s(f"{name}_pow"), 2)
                nc.vector.tensor_scalar(pw[:, 2, :].bitcast(I32), pw[:, 1, :].bitcast(I32), 0x7F800000, None,
                                        ALU.bitwise_and).then_inc(s(f"{name}_pow"), 1)

            nc.vector.memset(ones[:, :], 1.0).then_inc(s("l_init"), 1)
            norm(0, largest, lambda: power("c", cpow, bank[3], KTOP))
            dve.wait_ge(s("c_bc"), 1)
            nc.vector.reciprocal(csc[:, :, 0], bank[3][:, 256:258]).then_inc(s("c_scale"), 1)
            nc.vector.tensor_scalar(csc[:, :, 1], bank[3][:, 256:258], 2.0 ** (KTOP - ZTOP) / SSCALE, None,
                                    ALU.mult).then_inc(s("c_scale"), 1)

            def split_taps(l):
                dve.wait_ge(s("c_scale"), 2)
                nc.vector.tensor_scalar(samp[l][:, 0, :], samw[l][:, :], csc[:, l, 0:1], None, ALU.mult)\
                    .then_inc(s(f"c{l}_taps"), 1)
                dve.wait_ge(s(f"c{l}_taps"), 1)
                nc.vector.scalar_tensor_tensor(out=samp[l][:, 1, :], in0=samw[l][:, :], scalar=csc[:, l, 0:1],
                                               in1=samp[l][:, 0, :], op0=ALU.mult, op1=ALU.subtract)\
                    .then_inc(s(f"c{l}_taps"), 1)

            dve.wait_ge(s("bn_a"), 1)
            nc.vector.reciprocal(bnw[:, 1:2], bnw[:, 0:1]).then_inc(s("bn_d"), 1)
            dve.wait_ge(s("bn_d"), 1)
            nc.vector.tensor_tensor(bnw[:, 2:3], bnw[:, 1:2], bnp[:, 0:1], ALU.mult).then_inc(s("bn_d"), 1)
            nc.vector.tensor_tensor(bnw[:, 3:4], bnp[:, 4:5], bnp[:, 2:3], ALU.subtract).then_inc(s("bn_d"), 1)
            dve.wait_ge(s("bn_d"), 3)
            nc.vector.tensor_tensor(bnw[:, 5:6], bnw[:, 3:4], bnw[:, 2:3], ALU.mult).then_inc(s("bn_d"), 1)
            dve.wait_ge(s("bn_d"), 4)
            nc.vector.tensor_tensor(bnw[:, 4:5], bnw[:, 5:6], bnp[:, 1:2], ALU.add).then_inc(s("bn_d"), 1)
            dve.wait_ge(s("c_scale"), 2)
            nc.vector.tensor_tensor(bnw[:, 0:1], bnw[:, 2:3], csc[:, 0, 1:2], ALU.mult).then_inc(s("bn_d"), 1)
            dve.wait_ge(s("ld_const"), 32)
            conv(0)
            dve.wait_ge(s("ld_w13"), 16 * 2 * PAIRS)
            nc.vector.tensor_reduce(wmax[:, 0:1], w13s[:, :, :].rearrange("p e n -> p (e n)"), AX.X, ALU.max,
                                    apply_absolute_value=True).then_inc(s("w_max"), 1)
            dve.wait_ge(s("ld_w2"), 16 * PAIRS)
            nc.vector.tensor_reduce(wmax[:, 1:2], w2f[:, :, :, :].rearrange("p e a c -> p (e a c)"), AX.X, ALU.max,
                                    apply_absolute_value=True).then_inc(s("w_max"), 1)

            norm(1)
            nc.vector.memset(hr[:, SLOTS - 1, :], 0.0).then_inc(s("l_init"), 1)
            nc.vector.memset(gate_i[:, :, :], 0.0).then_inc(s("l_init"), 1)
            nc.vector.memset(cell[:, :, :], 0.0).then_inc(s("l_init"), 1)
            nc.vector.memset(xn[:, COLS:COLS + T], 0.0).then_inc(s("l_h"), 1)
            power("w", wpow, bank[4], WTOP)
            dve.wait_ge(s("w_bc"), 1)
            nc.vector.reciprocal(wsc[:, 0:2], bank[5][:, 0:2]).then_inc(s("w_scale"), 1)
            nc.vector.tensor_copy(wsc[:, 2:4], bank[5][:, 0:2]).then_inc(s("w_scale"), 1)
            dve.wait_ge(s("w_scale"), 2)
            nc.vector.tensor_scalar(wsc[:, 4:5], wsc[:, 2:3], 1 / XSCALE, None, ALU.mult).then_inc(s("w_fac"), 1)
            nc.vector.tensor_scalar(wsc[:, 5:6], wsc[:, 0:1], HSCALE / XSCALE / 4.0 ** WTOP, None, ALU.mult)\
                .then_inc(s("w_fac"), 1)
            nc.vector.scalar_tensor_tensor(out=wsc[:, 6:7], in0=wsc[:, 2:3], scalar=4.0 ** WTOP / HSCALE,
                                           in1=wsc[:, 2:3], op0=ALU.mult, op1=ALU.mult).then_inc(s("w_fac"), 1)
            dve.wait_ge(s("w_fac"), 3)
            nc.vector.tensor_tensor(wsc[:, 7:8], wsc[:, 6:7], wsc[:, 3:4], ALU.mult).then_inc(s("w_fac"), 1)
            dve.wait_ge(s("l_init"), 4)
            with dve.Fori(0, H // ROWS) as i:
                for q in range(ROWS):
                    dve.wait_ge(s("l_res"), ROWS * i + q + 1)
                    for t in range(W):
                        slot = q * W + t
                        step = dve.snap(SLOTS * i + slot + 1)
                        dve.wait_ge(s("l_h"), step)
                        nc.vector.tensor_tensor(cand[:, :, 1], hr[:, (slot - 1) % SLOTS, :],
                                                cell[:, :, 1], ALU.mult).then_inc(s("l_hc"), 1)
                        dve.wait_ge(s("l_act"), step)
                        dve.wait_ge(s("l_hc"), step)
                        nc.vector.tensor_tensor_scan(cell[:, :, :].rearrange("p b k -> p (b k)"),
                                                     gate_i[:, :, :].rearrange("p b k -> p (b k)"),
                                                     cand[:, :, :].rearrange("p b k -> p (b k)"), 0.0,
                                                     ALU.mult, ALU.add).then_inc(s("l_c"), 1)
                        dve.wait_ge(s("l_oact"), step)
                        dve.wait_ge(s("l_tc"), step)
                        nc.vector.tensor_tensor(hr[:, slot, :], og[:, :], tcell[:, :], ALU.mult)\
                            .then_inc(s("l_h"), 1)

            norm(2)
            conv(1)

            dve.sem_inc(s("m_hid"), 2)
            dve.sem_inc(s("m_acc"), 4)
            norm(3)
            def col(k):
                return gt[:, k, :, :]

            def wide(a):
                return a.unsqueeze(2).broadcast_to([P, 16, E])

            red = [small[:, k, :] for k in range(8)]
            sm = [0]

            def note(ins):
                sm[0] += 1
                ins.then_inc(s("m_sm"), 1)
                dve.wait_ge(s("m_sm"), sm[0])

            rank = rank_c[:, :].unsqueeze(1).broadcast_to([P, 16, E])
            dve.wait_ge(s("m_log"), 1)
            logits = bank[6][:, 0:128].rearrange("p (g e) -> p g e", e=E)
            nc.vector.reduce_max(red[0], logits, AX.X).then_inc(s("m_max"), 1)
            dve.wait_ge(s("m_max"), 1)
            nc.vector.tensor_tensor(col(1), logits, wide(red[0]), ALU.subtract).then_inc(s("m_max"), 1)
            dve.wait_ge(s("m_exp"), 1)
            note(nc.vector.reduce_sum(red[1], col(0), AX.X))
            note(nc.vector.reciprocal(red[2], red[1]))
            note(nc.vector.tensor_tensor(col(2), col(0), wide(red[2]), ALU.mult))
            note(nc.vector.reduce_max(red[3], col(2), AX.X))
            note(nc.vector.tensor_tensor(col(3), col(2), wide(red[3]), ALU.is_equal))
            note(nc.vector.tensor_tensor(col(4), col(3), rank, ALU.mult))
            note(nc.vector.reduce_max(red[4], col(4), AX.X))
            note(nc.vector.tensor_tensor(col(5), col(4), wide(red[4]), ALU.is_equal))
            note(nc.vector.scalar_tensor_tensor(out=col(6), in0=col(5), scalar=-2.0, in1=col(2),
                                                op0=ALU.mult, op1=ALU.add))
            note(nc.vector.reduce_max(red[5], col(6), AX.X))
            note(nc.vector.tensor_tensor(col(3), col(6), wide(red[5]), ALU.is_equal))
            note(nc.vector.tensor_tensor(col(4), col(3), rank, ALU.mult))
            note(nc.vector.reduce_max(red[4], col(4), AX.X))
            note(nc.vector.tensor_tensor(col(7), col(4), wide(red[4]), ALU.is_equal))
            note(nc.vector.scalar_tensor_tensor(out=red[6], in0=red[3], scalar=1e-9, in1=red[5],
                                                op0=ALU.add, op1=ALU.add))
            note(nc.vector.reciprocal(red[7], red[6]))
            note(nc.vector.tensor_tensor(col(5), col(5), wide(red[3]), ALU.mult))
            note(nc.vector.tensor_tensor(col(7), col(7), wide(red[5]), ALU.mult))
            note(nc.vector.tensor_tensor(col(5), col(5), col(7), ALU.add))
            note(nc.vector.tensor_tensor(g1[:, :, :, :].rearrange("p j h e -> p (j h) e"), col(5),
                                         wide(red[7]), ALU.mult))
            note(nc.vector.tensor_scalar(g1[:, :, :, :], g1[:, :, :, :], wsc[:, 7:8], None, ALU.mult))
            dve.wait_ge(s("m_zero"), 1)
            U = 2 * NCH * PT
            with dve.Fori(0, PAIRS // 2) as i:
                def gather(g, n):
                    k = n // 2
                    dve.wait_ge(s("m_y"), 2 * NCH * i + g + 1)
                    dve.wait_ge(s("m_acc"), 4 * NCH * i + 2 * g + k + 4)
                    for jj in range(n % 2 * 2, n % 2 * 2 + 2):
                        j, hf = g % 2 * JJ + jj, g // 2 % 2
                        mm = nc.vector.scalar_tensor_tensor(
                            out=acc[:, j, hf, :],
                            in0=bank[4 + 2 * (g % 2) + jj // 2][:, (2 * (jj % 2) + k) * 128:][:, 0:128],
                            scalar=ge[:, g // NCH, j, hf, k:k + 1], in1=acc[:, j, hf, :],
                            op0=ALU.mult, op1=ALU.add)
                    if n % 2 == 1:
                        mm.then_inc(s("m_acc"), 1)

                dve.wait_ge(s("m_acc"), 4 * NCH * i + 4)
                for q in range(2):
                    nc.vector.tensor_copy(ge[:, q, :, :, :], g1[:, :, :, bass.ds(4 * i + 2 * q, 2)])\
                        .then_inc(s("m_ge"), 1)
                dve.wait_ge(s("m_ge"), 2 * i + 2)
                for u in range(U):
                    dve.wait_ge(s("m_silu"), U * i + u + 1)
                    dve.wait_ge(s("m_h"), 2 * U * i + 2 * u + 2)
                    nc.vector.scalar_tensor_tensor(out=hid[:, u % MR, :], in0=bank[2 + u % 2][:, :],
                                                   scalar=wsc[:, 5:6], in1=silu[:, u % 2, :],
                                                   op0=ALU.mult, op1=ALU.mult).then_inc(s("m_hid"), 1)
                    if MLAG <= u % PT < MLAG + 4 and u > PT:
                        gather(u // PT - 1, u % PT - MLAG)
                for n in range(4):
                    gather(2 * NCH - 1, n)
            dve.wait_ge(s("m_acc"), 4 + 2 * NCH * PAIRS)
            parts = acc.rearrange("p j h (k c) -> p (j h) k c", k=2)
            for q in range(2):
                half = slice(8 * q, 8 * q + 8)
                nc.vector.tensor_tensor(sq[:, q * 512:q * 512 + 512].rearrange("p (g c) -> p g c", c=C),
                                        parts[:, half, 0, :], parts[:, half, 1, :], ALU.add).then_inc(s("m_sum"), 1)
            for q in range(2):
                dve.wait_ge(s("m_tr"), q + 1)
                nc.vector.tensor_tensor(xs[:, q * 512:q * 512 + 512], xs[:, q * 512:q * 512 + 512],
                                        bank[6 + q][:, :], ALU.add).then_inc(s("m_out"), 1)


def kernel(**inputs):
    import numpy as np
    import concourse.bacc as bacc
    from concourse.bass_utils import run_bass_kernel_spmd

    a = {k: np.asarray(v) for k, v in inputs.items()}
    f = np.float32

    q = np.arange(P)
    pos = np.arange(16)
    tap = np.arange(TAPS)
    cy = 8 * np.arange(2)[None, :, None, None] + (q // W)[:, None, None, None] - 1 \
        + (tap // 3)[None, None, :, None] - pos
    cx = 0 * cy + (q % W)[:, None, None, None] - 1 + (tap % 3)[None, None, :, None] - pos
    tents = np.stack([cy, cx], 2).reshape(P, -1)
    mean = np.kron(np.eye(2), np.ones((C, C))) / C
    rank = np.tile(E - np.arange(E), (P, 1))
    consts = np.concatenate([mean, np.eye(P), rank, tents], 1).astype(f)

    def halves(t, fill):
        return np.stack([np.concatenate([t, fill], 0), np.concatenate([fill, t], 0)], 1)

    def conv_weights(w, order):
        w = w[order]
        main = np.stack([w[:, :, ky, kx] for ky in range(3) for kx in (0, 2)], 0)
        zero = np.zeros_like(w[:, :, 0, 0])
        side = np.stack([t for ky in range(3) for t in (w[:, :, ky, 1], zero)], 0)
        return halves(main.transpose(2, 0, 1), side.transpose(2, 0, 1))

    def sample_weights(w):
        t = w.transpose(1, 2, 3, 0).reshape(C, TAPS * C)
        return np.concatenate([t, t], 0)

    split_yx = list(range(27))
    pairs_yx = list(range(0, 18, 2)) + list(range(1, 18, 2)) + list(range(18, 27))
    conv_w = np.stack([conv_weights(a["L0_conv_w_off"], split_yx), conv_weights(a["L1_conv_offset_w"], pairs_yx)])
    conv_b = np.stack([a["L0_conv_b_off"], a["L1_conv_offset_b"][pairs_yx]], 1)
    sample_w = np.stack([sample_weights(a["L0_conv_w"]), sample_weights(a["L1_conv_dcn_w"])])
    bn = np.stack([a["L0_conv_" + k] for k in ("gamma", "beta", "run_mean", "run_var", "b", "b")], 1)
    bn = np.concatenate([bn, bn], 0)
    gates = ("c", "i", "o")
    u = np.concatenate([a["L0_ffn_U_" + k] for k in gates], 1)
    lstm_u = halves(u, np.zeros_like(u))
    lstm_v = np.concatenate([a["L0_ffn_V_" + k] for k in gates], 1)
    lstm_b = np.concatenate([a["L0_ffn_b_" + k] for k in gates])[None]
    router = np.zeros((P, 2, E), f)
    router[:C, 0], router[C:, 1] = a["L1_ffn_router_w"].T, a["L1_ffn_router_w"].T
    full = FT * 128
    w13 = np.zeros((PAIRS, C, 2, PH), f)
    w2 = np.zeros((PAIRS, W2B, 128, C), f)
    for e in range(E):
        pr, k = e // 2, e % 2
        tail = 2 * full + k * REST
        for m, name in enumerate(("w1", "w3")):
            w = a["L1_ffn_" + name][e].T
            w13[pr, :, m, k * full:(k + 1) * full] = w[:, :full]
            w13[pr, :, m, tail:tail + REST] = w[:, full:]
        w = a["L1_ffn_w2"][e].T
        w2[pr, k * FT:(k + 1) * FT] = w[:full].reshape(FT, 128, C)
        w2[pr, 2 * FT + k, k * REST:(k + 1) * REST] = w[full:]
    w2 = w2.transpose(0, 2, 1, 3).reshape(PAIRS, 128, W2B * C)

    arrays = dict(x=a["x"], consts=consts, conv_w=conv_w, conv_b=conv_b, sample_w=sample_w, bn=bn,
                  lstm_u=lstm_u, lstm_v=lstm_v, lstm_b=lstm_b, router=router.reshape(P, 2 * E),
                  w13=w13.reshape(PAIRS, C, 2 * PH), w2=w2)
    arrays = {k: np.ascontiguousarray(v) for k, v in arrays.items()}
    nc = bacc.Bacc("TRN2", target_bir_lowering=False, num_devices=1)
    dram = {k: nc.dram_tensor(k, v.shape, F32, kind="ExternalInput").ap() for k, v in arrays.items()}
    out = nc.dram_tensor("out", (B, C, H, W), F32, kind="ExternalOutput").ap()
    split = lambda t: t.rearrange("(h b) c y x -> h c b (y x)", h=2)
    build(nc, split(dram["x"]), *[dram[k] for k in list(arrays)[1:]], split(out))
    r = run_bass_kernel_spmd(nc, [arrays], core_ids=[0])
    return r.results[0]["out"]
```
